# Optimizing a Trainium2 kernel written in Bass

```python
import numpy as np
import jax
import jax.numpy as jnp

def _softmax(x, axis=-1):
    return jax.nn.softmax(x, axis=axis)

def _gelu(x):
    return jax.nn.gelu(x, approximate=True)

def _silu(x):
    return jax.nn.silu(x)

def _sigmoid(x):
    return jax.nn.sigmoid(x)

def _layernorm(x, axis=-1, eps=1e-05):
    m = jnp.mean(x, axis=axis, keepdims=True)
    v = jnp.var(x, axis=axis, keepdims=True)
    return (x - m) / jnp.sqrt(v + eps)

def _scatter_add(tgt, idx, src, axis=0):
    return tgt.at[idx].add(src)

def _segment_sum(src, seg, n):
    return jax.ops.segment_sum(src, seg, n)
kernel_name = 'mk_decoder_preln_d2_seqx_r4_ead6bf'

def setup_inputs(seed: int=0):
    np.random.seed(seed)
    _w = jnp.asarray

    def _rec_inputs():
        import jax
        import jax.numpy as jnp
        _rk = jax.random.key(seed)
        x = 7.22e-05 + 1 * jax.random.normal(jax.random.fold_in(_rk, 1), (2, 512, 256), jnp.float32)
        _lenS = 512 - jax.random.randint(jax.random.fold_in(_rk, 7), (2,), 0, max(1, 512 // 4) + 1, jnp.int32)
        _lenS2 = 1024 - jax.random.randint(jax.random.fold_in(_rk, 8), (2,), 0, max(1, 1024 // 4) + 1, jnp.int32)
        _ctx_768P = jax.random.normal(jax.random.fold_in(_rk, 11), (2, 16, 192), jnp.float32)
        _ctx_768c = jax.random.dirichlet(jax.random.fold_in(_rk, 511), 0.3 * jnp.ones((16,), jnp.float32), (2, 1024))
        _ctx_768t = jnp.einsum('bsk,bkd->bsd', _ctx_768c, _ctx_768P)
        _ctx_768t = _ctx_768t * jax.lax.rsqrt(jnp.mean(jnp.square(_ctx_768t)) + 1e-12) * 0.953939
        ctx_768 = -0.000191848 + 0.999787 * (_ctx_768t + 0.3 * jax.random.normal(jax.random.fold_in(_rk, 611), (2, 1024, 192), jnp.float32))
        return (x, ctx_768)
    x, ctx_768 = _rec_inputs()

    def _L0_attn_setup():
        import jax, jax.numpy as jnp
        import numpy as np
        T, B, E = (512, 16, 256)
        CDIM = 256
        H = 16
        K = 31

        def _xavier(k, shape):
            fan_out, fan_in = shape
            lim = float(np.sqrt(6.0 / (fan_in + fan_out)))
            return jax.random.uniform(k, shape, jnp.float32, -lim, lim)

        def layer_norm(x, g, b, eps=1e-05):
            m = x.mean(-1, keepdims=True)
            v = ((x - m) ** 2).mean(-1, keepdims=True)
            return (x - m) * jax.lax.rsqrt(v + eps) * g + b

        def dynamic_conv(h, ww, bw):
            Tn, Bn, C = h.shape
            R = C // H
            w = jax.nn.softmax((h @ ww.T + bw).reshape(Tn, Bn, H, K), axis=-1)
            hp = jnp.pad(h.reshape(Tn, Bn, H, R), ((K - 1, 0), (0, 0), (0, 0), (0, 0)))
            acc = jnp.zeros((Tn, Bn, H, R), h.dtype)
            for k in range(K):
                acc = acc + w[:, :, :, k:k + 1] * hp[k:k + Tn]
            return acc.reshape(Tn, Bn, C)
        key = jax.random.key(seed)
        ks = jax.random.split(key, 5)
        return {'x': jax.random.normal(ks[0], (T, B, E), jnp.float32), 'w1': _xavier(ks[1], (CDIM, E)), 'b1': jnp.zeros((CDIM,), jnp.float32), 'ww': _xavier(ks[2], (H * K, CDIM)), 'bw': jnp.zeros((H * K,), jnp.float32), 'w2': _xavier(ks[3], (E, CDIM)), 'b2': jnp.zeros((E,), jnp.float32), 'gamma': jnp.ones((E,), jnp.float32), 'beta': jnp.zeros((E,), jnp.float32)}
    _L0_attn_all = _L0_attn_setup()
    _L0_attn_in = {k: v for k, v in _L0_attn_all.items() if k in ('w1', 'b1', 'ww', 'bw', 'w2', 'b2', 'gamma', 'beta')}
    del _L0_attn_all

    def _L0_xattn_setup():
        import jax, jax.numpy as jnp
        import numpy as np
        DIM = 256
        CTX_DIM = 192
        H = 16
        DH = 64
        INNER = H * DH
        EPS = 1e-05

        def layer_norm(x, gamma, beta):
            mu = jnp.mean(x, axis=-1, keepdims=True)
            var = jnp.mean(jnp.square(x - mu), axis=-1, keepdims=True)
            return (x - mu) * jax.lax.rsqrt(var + EPS) * gamma + beta
        key = jax.random.key(seed)
        ks = jax.random.split(key, 8)
        B, N, M = (4, 512, 512)
        x = jax.random.normal(ks[0], (B, N, DIM), dtype=jnp.float32)
        context = jax.random.normal(ks[1], (B, M, CTX_DIM), dtype=jnp.float32)
        g_x = jnp.ones((DIM,), jnp.float32)
        b_x = jnp.zeros((DIM,), jnp.float32)
        g_c = jnp.ones((CTX_DIM,), jnp.float32)
        b_c = jnp.zeros((CTX_DIM,), jnp.float32)
        Wq = jax.random.normal(ks[2], (DIM, INNER), dtype=jnp.float32) / np.sqrt(DIM)
        Wk = jax.random.normal(ks[3], (CTX_DIM, INNER), dtype=jnp.float32) / np.sqrt(CTX_DIM)
        Wv = jax.random.normal(ks[4], (CTX_DIM, INNER), dtype=jnp.float32) / np.sqrt(CTX_DIM)
        Wo = jax.random.normal(ks[5], (INNER, DIM), dtype=jnp.float32) / np.sqrt(INNER)
        return {'x': x, 'context': context, 'g_x': g_x, 'b_x': b_x, 'g_c': g_c, 'b_c': b_c, 'Wq': Wq, 'Wk': Wk, 'Wv': Wv, 'Wo': Wo}
    _L0_xattn_all = _L0_xattn_setup()
    _L0_xattn_in = {k: v for k, v in _L0_xattn_all.items() if k in ('g_x', 'b_x', 'g_c', 'b_c', 'Wq', 'Wk', 'Wv', 'Wo')}
    del _L0_xattn_all

    def _L0_ffn_setup():
        import jax, jax.numpy as jnp
        import numpy as np
        B, S, H = (2, 256, 256)
        KD, NH, K = (128, 8, 8)
        NE = 16384
        NK = 64
        EPS = 1e-05
        key = jax.random.key(seed)
        ks = jax.random.split(key, 5)
        inputs = jax.random.normal(ks[0], (B, S, H), jnp.float32)
        bn_gamma = jnp.ones((H,), jnp.float32)
        bn_beta = jnp.zeros((H,), jnp.float32)
        w_q = jax.random.normal(ks[1], (2 * NH * KD, H), jnp.float32) * (1.0 / np.sqrt(H))
        keys_p = jax.random.normal(ks[2], (NH, NK, 2, KD), jnp.float32) * 0.02
        lim = float(np.sqrt(6.0 / (NE + H)))
        down = jax.random.uniform(ks[3], (NE, H), jnp.float32, -lim, lim)
        up = jax.random.uniform(ks[4], (NE, H), jnp.float32, -lim, lim)
        return {'inputs': inputs, 'bn_gamma': bn_gamma, 'bn_beta': bn_beta, 'w_q': w_q, 'keys_p': keys_p, 'down': down, 'up': up}
    _L0_ffn_all = _L0_ffn_setup()
    _L0_ffn_in = {k: v for k, v in _L0_ffn_all.items() if k in ('bn_gamma', 'bn_beta', 'w_q', 'keys_p', 'down', 'up')}
    del _L0_ffn_all

    def _L1_attn_setup():
        import jax, jax.numpy as jnp
        import numpy as np
        D = 256
        FF = 1024
        EPS = 1e-06

        def _linear(x, w, b):
            return jnp.einsum('bld,fd->blf', x, w) + b

        def _rmsnorm(x, g):
            xf = x.astype(jnp.float32)
            out = xf * jax.lax.rsqrt(jnp.mean(xf * xf, axis=-1, keepdims=True) + EPS)
            return out.astype(x.dtype) * g

        def _silu(x):
            return x * jax.nn.sigmoid(x)
        key = jax.random.key(seed)
        ks = jax.random.split(key, 20)
        sd = 1.0 / np.sqrt(D)
        sf = 1.0 / np.sqrt(FF)
        inp = {'x': jax.random.normal(ks[0], (4, 1024, D), jnp.float32), 'w_ln_z': jax.random.uniform(ks[1], (D, D), jnp.float32, -sd, sd), 'b_ln_z': jax.random.uniform(ks[2], (D,), jnp.float32, -sd, sd), 'w_dt': jax.random.uniform(ks[3], (D, D), jnp.float32, -sd, sd), 'b_dt': jax.random.uniform(ks[4], (D,), jnp.float32, -sd, sd), 'w_y': jax.random.uniform(ks[5], (D, D), jnp.float32, -sd, sd), 'b_y': jax.random.uniform(ks[6], (D,), jnp.float32, -sd, sd), 'w_yact': jax.random.uniform(ks[7], (D, D), jnp.float32, -sd, sd), 'b_yact': jax.random.uniform(ks[8], (D,), jnp.float32, -sd, sd), 'h0': jax.random.normal(ks[9], (D,), jnp.float32), 'w_fc': jax.random.uniform(ks[10], (FF, D), jnp.float32, -sd, sd), 'b_fc': jax.random.uniform(ks[11], (FF,), jnp.float32, -sd, sd), 'w_fcact': jax.random.uniform(ks[12], (FF, D), jnp.float32, -sd, sd), 'b_fcact': jax.random.uniform(ks[13], (FF,), jnp.float32, -sd, sd), 'w_out': jax.random.uniform(ks[14], (D, FF), jnp.float32, -sf, sf), 'b_out': jax.random.uniform(ks[15], (D,), jnp.float32, -sf, sf), 'g_sio': jnp.ones((D,), jnp.float32), 'g_ffn': jnp.ones((D,), jnp.float32)}
        return inp
    _L1_attn_all = _L1_attn_setup()
    _L1_attn_in = {k: v for k, v in _L1_attn_all.items() if k in ('w_ln_z', 'b_ln_z', 'w_dt', 'b_dt', 'w_y', 'b_y', 'w_yact', 'b_yact', 'h0', 'w_fc', 'b_fc', 'w_fcact', 'b_fcact', 'w_out', 'b_out', 'g_sio', 'g_ffn')}
    del _L1_attn_all

    def _L1_xattn_setup():
        import jax, jax.numpy as jnp
        import numpy as np
        NUM_HEADS = 16
        key = jax.random.key(seed)
        ks = jax.random.split(key, 8)
        dim, cond_dim = (256, 192)
        B, N, condN = (4, 512, 256)
        s = lambda k, shp, fan: jax.random.normal(k, shp, dtype=jnp.float32) * fan ** (-0.5)
        return {'x': jax.random.normal(ks[0], (B, N, dim), dtype=jnp.float32), 'cond': jax.random.normal(ks[1], (B, condN, cond_dim), dtype=jnp.float32), 'q_w': s(ks[2], (dim, dim), dim), 'q_b': jnp.zeros((dim,), jnp.float32), 'kv_w': s(ks[3], (cond_dim, 2 * dim), cond_dim), 'kv_b': jnp.zeros((2 * dim,), jnp.float32), 'proj_w': s(ks[4], (dim, dim), dim), 'proj_b': jnp.zeros((dim,), jnp.float32)}
    _L1_xattn_all = _L1_xattn_setup()
    _L1_xattn_in = {k: v for k, v in _L1_xattn_all.items() if k in ('q_w', 'q_b', 'kv_w', 'kv_b', 'proj_w', 'proj_b')}
    del _L1_xattn_all

    def _L1_ffn_setup():
        import jax, jax.numpy as jnp
        import numpy as np
        DIM = 256
        HEADS = 16
        HD = DIM // HEADS
        M = 64
        E = 4
        K = 2
        HID = 512
        MID = 512
        LB = 0.01
        EPS = 1.1920929e-07

        def _rms(x, w):
            return x * jax.lax.rsqrt(jnp.mean(x * x, axis=-1, keepdims=True) + EPS) * w

        def _gelu(x):
            return jax.nn.gelu(x, approximate=False)
        key = jax.random.key(seed)
        ks = jax.random.split(key, 20)
        d = DIM
        w = lambda k, s: jax.random.normal(k, s, jnp.float32) * 0.02
        return {'x': jax.random.normal(ks[0], (4, 256, d), jnp.float32), 'n1_w': jnp.ones((d,), jnp.float32), 'n2_w': jnp.ones((d,), jnp.float32), 'wq': w(ks[1], (d, d)), 'wk': w(ks[2], (d, d)), 'wv': w(ks[3], (d, d)), 'wo': w(ks[4], (d, d)), 'qn_w': jnp.ones((HD,), jnp.float32), 'kn_w': jnp.ones((HD,), jnp.float32), 'gate_w': w(ks[5], (E, d)), 'e0_up': w(ks[6], (HID, d)), 'e0_down': w(ks[7], (d, HID)), 'e1_w1': w(ks[8], (HID, d)), 'e1_w2': w(ks[9], (HID, d)), 'e1_down': w(ks[10], (d, HID)), 'e2_l1': w(ks[11], (MID, d)), 'e2_l2': w(ks[12], (HID, MID)), 'e2_l3': w(ks[13], (MID, HID)), 'e2_l4': w(ks[14], (d, MID)), 'e3_down': w(ks[15], (d, d)), 'e3_up': w(ks[16], (HID, d)), 'e3_out': w(ks[17], (d, HID))}
    _L1_ffn_all = _L1_ffn_setup()
    _L1_ffn_in = {k: v for k, v in _L1_ffn_all.items() if k in ('n1_w', 'n2_w', 'wq', 'wk', 'wv', 'wo', 'qn_w', 'kn_w', 'gate_w', 'e0_up', 'e0_down', 'e1_w1', 'e1_w2', 'e1_down', 'e2_l1', 'e2_l2', 'e2_l3', 'e2_l4', 'e3_down', 'e3_up', 'e3_out')}
    del _L1_ffn_all
    return {'x': x, 'ctx_768': ctx_768, 'L0_attn_w1': _L0_attn_in['w1'], 'L0_attn_b1': _L0_attn_in['b1'], 'L0_attn_ww': _L0_attn_in['ww'], 'L0_attn_bw': _L0_attn_in['bw'], 'L0_attn_w2': _L0_attn_in['w2'], 'L0_attn_b2': _L0_attn_in['b2'], 'L0_attn_gamma': _L0_attn_in['gamma'], 'L0_attn_beta': _L0_attn_in['beta'], 'L0_xattn_g_x': _L0_xattn_in['g_x'], 'L0_xattn_b_x': _L0_xattn_in['b_x'], 'L0_xattn_g_c': _L0_xattn_in['g_c'], 'L0_xattn_b_c': _L0_xattn_in['b_c'], 'L0_xattn_Wq': _L0_xattn_in['Wq'], 'L0_xattn_Wk': _L0_xattn_in['Wk'], 'L0_xattn_Wv': _L0_xattn_in['Wv'], 'L0_xattn_Wo': _L0_xattn_in['Wo'], 'L0_ffn_bn_gamma': _L0_ffn_in['bn_gamma'], 'L0_ffn_bn_beta': _L0_ffn_in['bn_beta'], 'L0_ffn_w_q': _L0_ffn_in['w_q'], 'L0_ffn_keys_p': _L0_ffn_in['keys_p'], 'L0_ffn_down': _L0_ffn_in['down'], 'L0_ffn_up': _L0_ffn_in['up'], 'L1_attn_w_ln_z': _L1_attn_in['w_ln_z'], 'L1_attn_b_ln_z': _L1_attn_in['b_ln_z'], 'L1_attn_w_dt': _L1_attn_in['w_dt'], 'L1_attn_b_dt': _L1_attn_in['b_dt'], 'L1_attn_w_y': _L1_attn_in['w_y'], 'L1_attn_b_y': _L1_attn_in['b_y'], 'L1_attn_w_yact': _L1_attn_in['w_yact'], 'L1_attn_b_yact': _L1_attn_in['b_yact'], 'L1_attn_h0': _L1_attn_in['h0'], 'L1_attn_w_fc': _L1_attn_in['w_fc'], 'L1_attn_b_fc': _L1_attn_in['b_fc'], 'L1_attn_w_fcact': _L1_attn_in['w_fcact'], 'L1_attn_b_fcact': _L1_attn_in['b_fcact'], 'L1_attn_w_out': _L1_attn_in['w_out'], 'L1_attn_b_out': _L1_attn_in['b_out'], 'L1_attn_g_sio': _L1_attn_in['g_sio'], 'L1_attn_g_ffn': _L1_attn_in['g_ffn'], 'L1_xattn_q_w': _L1_xattn_in['q_w'], 'L1_xattn_q_b': _L1_xattn_in['q_b'], 'L1_xattn_kv_w': _L1_xattn_in['kv_w'], 'L1_xattn_kv_b': _L1_xattn_in['kv_b'], 'L1_xattn_proj_w': _L1_xattn_in['proj_w'], 'L1_xattn_proj_b': _L1_xattn_in['proj_b'], 'L1_ffn_n1_w': _L1_ffn_in['n1_w'], 'L1_ffn_n2_w': _L1_ffn_in['n2_w'], 'L1_ffn_wq': _L1_ffn_in['wq'], 'L1_ffn_wk': _L1_ffn_in['wk'], 'L1_ffn_wv': _L1_ffn_in['wv'], 'L1_ffn_wo': _L1_ffn_in['wo'], 'L1_ffn_qn_w': _L1_ffn_in['qn_w'], 'L1_ffn_kn_w': _L1_ffn_in['kn_w'], 'L1_ffn_gate_w': _L1_ffn_in['gate_w'], 'L1_ffn_e0_up': _L1_ffn_in['e0_up'], 'L1_ffn_e0_down': _L1_ffn_in['e0_down'], 'L1_ffn_e1_w1': _L1_ffn_in['e1_w1'], 'L1_ffn_e1_w2': _L1_ffn_in['e1_w2'], 'L1_ffn_e1_down': _L1_ffn_in['e1_down'], 'L1_ffn_e2_l1': _L1_ffn_in['e2_l1'], 'L1_ffn_e2_l2': _L1_ffn_in['e2_l2'], 'L1_ffn_e2_l3': _L1_ffn_in['e2_l3'], 'L1_ffn_e2_l4': _L1_ffn_in['e2_l4'], 'L1_ffn_e3_down': _L1_ffn_in['e3_down'], 'L1_ffn_e3_up': _L1_ffn_in['e3_up'], 'L1_ffn_e3_out': _L1_ffn_in['e3_out']}

def reference(x, ctx_768, L0_attn_w1, L0_attn_b1, L0_attn_ww, L0_attn_bw, L0_attn_w2, L0_attn_b2, L0_attn_gamma, L0_attn_beta, L0_xattn_g_x, L0_xattn_b_x, L0_xattn_g_c, L0_xattn_b_c, L0_xattn_Wq, L0_xattn_Wk, L0_xattn_Wv, L0_xattn_Wo, L0_ffn_bn_gamma, L0_ffn_bn_beta, L0_ffn_w_q, L0_ffn_keys_p, L0_ffn_down, L0_ffn_up, L1_attn_w_ln_z, L1_attn_b_ln_z, L1_attn_w_dt, L1_attn_b_dt, L1_attn_w_y, L1_attn_b_y, L1_attn_w_yact, L1_attn_b_yact, L1_attn_h0, L1_attn_w_fc, L1_attn_b_fc, L1_attn_w_fcact, L1_attn_b_fcact, L1_attn_w_out, L1_attn_b_out, L1_attn_g_sio, L1_attn_g_ffn, L1_xattn_q_w, L1_xattn_q_b, L1_xattn_kv_w, L1_xattn_kv_b, L1_xattn_proj_w, L1_xattn_proj_b, L1_ffn_n1_w, L1_ffn_n2_w, L1_ffn_wq, L1_ffn_wk, L1_ffn_wv, L1_ffn_wo, L1_ffn_qn_w, L1_ffn_kn_w, L1_ffn_gate_w, L1_ffn_e0_up, L1_ffn_e0_down, L1_ffn_e1_w1, L1_ffn_e1_w2, L1_ffn_e1_down, L1_ffn_e2_l1, L1_ffn_e2_l2, L1_ffn_e2_l3, L1_ffn_e2_l4, L1_ffn_e3_down, L1_ffn_e3_up, L1_ffn_e3_out):
    import jax
    import jax.numpy as jnp

    def _L0_attn_ref(x, w1, b1, ww, bw, w2, b2, gamma, beta):
        import jax, jax.numpy as jnp
        import numpy as np
        T, B, E = (512, 16, 256)
        CDIM = 256
        H = 16
        K = 31

        def _xavier(k, shape):
            fan_out, fan_in = shape
            lim = float(np.sqrt(6.0 / (fan_in + fan_out)))
            return jax.random.uniform(k, shape, jnp.float32, -lim, lim)

        def layer_norm(x, g, b, eps=1e-05):
            m = x.mean(-1, keepdims=True)
            v = ((x - m) ** 2).mean(-1, keepdims=True)
            return (x - m) * jax.lax.rsqrt(v + eps) * g + b

        def dynamic_conv(h, ww, bw):
            Tn, Bn, C = h.shape
            R = C // H
            w = jax.nn.softmax((h @ ww.T + bw).reshape(Tn, Bn, H, K), axis=-1)
            hp = jnp.pad(h.reshape(Tn, Bn, H, R), ((K - 1, 0), (0, 0), (0, 0), (0, 0)))
            acc = jnp.zeros((Tn, Bn, H, R), h.dtype)
            for k in range(K):
                acc = acc + w[:, :, :, k:k + 1] * hp[k:k + Tn]
            return acc.reshape(Tn, Bn, C)
        h = x @ w1.T + b1
        h = dynamic_conv(h, ww, bw)
        h = h @ w2.T + b2
        return layer_norm(x + h, gamma, beta)

    def _L0_xattn_ref(x, context, g_x, b_x, g_c, b_c, Wq, Wk, Wv, Wo):
        import jax, jax.numpy as jnp
        import numpy as np
        DIM = 256
        CTX_DIM = 192
        H = 16
        DH = 64
        INNER = H * DH
        EPS = 1e-05

        def layer_norm(x, gamma, beta):
            mu = jnp.mean(x, axis=-1, keepdims=True)
            var = jnp.mean(jnp.square(x - mu), axis=-1, keepdims=True)
            return (x - mu) * jax.lax.rsqrt(var + EPS) * gamma + beta
        B, N, _ = x.shape
        M = context.shape[1]
        xn = layer_norm(x, g_x, b_x)
        cn = layer_norm(context, g_c, b_c)
        q = (xn @ Wq).reshape(B, N, H, DH).transpose(0, 2, 1, 3)
        k = (cn @ Wk).reshape(B, M, H, DH).transpose(0, 2, 1, 3)
        v = (cn @ Wv).reshape(B, M, H, DH).transpose(0, 2, 1, 3)
        scale = jnp.float32(1.0 / np.sqrt(DH))
        sim = jnp.einsum('bhid,bhjd->bhij', q, k) * scale
        attn = jax.nn.softmax(sim, axis=-1)
        out = jnp.einsum('bhij,bhjd->bhid', attn, v)
        out = out.transpose(0, 2, 1, 3).reshape(B, N, INNER)
        return out @ Wo

    def _L0_ffn_ref(inputs, bn_gamma, bn_beta, w_q, keys_p, down, up):
        import jax, jax.numpy as jnp
        import numpy as np
        B, S, H = (2, 256, 256)
        KD, NH, K = (128, 8, 8)
        NE = 16384
        NK = 64
        EPS = 1e-05
        b, s, d = inputs.shape
        x = inputs.reshape(b * s, d)
        mean = x.mean(axis=0)
        var = x.var(axis=0)
        xn = (x - mean) * jax.lax.rsqrt(var + EPS) * bn_gamma + bn_beta
        xn = xn.reshape(b, s, d)
        q = (xn @ w_q.T).reshape(b, s, 2, NH, KD).transpose(2, 0, 1, 3, 4)
        sim = jnp.einsum('pbnhd,hkpd->pbnhk', q, keys_p)
        scores, idx = jax.lax.top_k(sim, K)
        all_scores = (scores[0][..., :, None] + scores[1][..., None, :]).reshape(b, s, NH, K * K)
        all_idx = (idx[0][..., :, None] * NK + idx[1][..., None, :]).reshape(b, s, NH, K * K)
        sc, pk = jax.lax.top_k(all_scores, K)
        indices = jnp.take_along_axis(all_idx, pk, axis=-1)
        wd = down[indices]
        hmid = jnp.einsum('bnd,bnhkd->bnhk', inputs, wd)
        hmid = jax.nn.sigmoid(sc) * jax.nn.gelu(hmid, approximate=False)
        wu = up[indices]
        return jnp.einsum('bnhk,bnhkd->bnd', hmid, wu)

    def _L1_attn_ref(x, w_ln_z, b_ln_z, w_dt, b_dt, w_y, b_y, w_yact, b_yact, h0, w_fc, b_fc, w_fcact, b_fcact, w_out, b_out, g_sio, g_ffn):
        import jax, jax.numpy as jnp
        import numpy as np
        D = 256
        FF = 1024
        EPS = 1e-06

        def _linear(x, w, b):
            return jnp.einsum('bld,fd->blf', x, w) + b

        def _rmsnorm(x, g):
            xf = x.astype(jnp.float32)
            out = xf * jax.lax.rsqrt(jnp.mean(xf * xf, axis=-1, keepdims=True) + EPS)
            return out.astype(x.dtype) * g

        def _silu(x):
            return x * jax.nn.sigmoid(x)
        xn = _rmsnorm(x, g_sio)
        ln_z = -jax.nn.softplus(-_linear(xn, w_ln_z, b_ln_z))
        dt = _linear(xn, w_dt, b_dt)
        ln_da = -jax.nn.softplus(-dt)
        ln_o_da = -jax.nn.softplus(dt)
        ln_o_da_cumsum = jnp.cumsum(ln_o_da, axis=1)
        lcse = jax.lax.cumlogsumexp(ln_z + ln_da - ln_o_da_cumsum, axis=1)
        h_inner = jnp.exp(lcse + ln_o_da_cumsum)
        h_cross = jnp.exp(ln_o_da_cumsum) * h0[None, None, :]
        h = h_inner + h_cross
        y = _linear(h, w_y, b_y) * _silu(_linear(xn, w_yact, b_yact))
        x = x + y
        xn2 = _rmsnorm(x, g_ffn)
        hid = _linear(xn2, w_fc, b_fc) * _silu(_linear(xn2, w_fcact, b_fcact))
        return x + _linear(hid, w_out, b_out)

    def _L1_xattn_ref(x, cond, q_w, q_b, kv_w, kv_b, proj_w, proj_b):
        import jax, jax.numpy as jnp
        import numpy as np
        NUM_HEADS = 16
        B, N, C = x.shape
        condN = cond.shape[1]
        H = NUM_HEADS
        hd = C // H
        scale = hd ** (-0.5)
        q = (x @ q_w + q_b).reshape(B, N, H, hd).transpose(0, 2, 1, 3)
        kv = (cond @ kv_w + kv_b).reshape(B, condN, 2, H, hd)
        k = kv[:, :, 0].transpose(0, 2, 1, 3)
        v = kv[:, :, 1].transpose(0, 2, 1, 3)
        attn = jnp.einsum('bhnd,bhmd->bhnm', q * scale, k)
        attn = jax.nn.softmax(attn, axis=-1)
        out = jnp.einsum('bhnm,bhmd->bhnd', attn, v)
        out = out.transpose(0, 2, 1, 3).reshape(B, N, C)
        return out @ proj_w + proj_b

    def _L1_ffn_ref(x, n1_w, n2_w, wq, wk, wv, wo, qn_w, kn_w, gate_w, e0_up, e0_down, e1_w1, e1_w2, e1_down, e2_l1, e2_l2, e2_l3, e2_l4, e3_down, e3_up, e3_out):
        import jax, jax.numpy as jnp
        import numpy as np
        DIM = 256
        HEADS = 16
        HD = DIM // HEADS
        M = 64
        E = 4
        K = 2
        HID = 512
        MID = 512
        LB = 0.01
        EPS = 1.1920929e-07

        def _rms(x, w):
            return x * jax.lax.rsqrt(jnp.mean(x * x, axis=-1, keepdims=True) + EPS) * w

        def _gelu(x):
            return jax.nn.gelu(x, approximate=False)
        B, T, C = x.shape
        h = _rms(x, n1_w)
        heads = lambda w_: (h @ w_.T).reshape(B, T, HEADS, HD).transpose(0, 2, 1, 3)
        q = _rms(heads(wq), qn_w)
        k = _rms(heads(wk), kn_w)
        v = heads(wv)
        scores = jnp.einsum('bhqd,bhkd->bhqk', q, k) * HD ** (-0.5)
        causal = jnp.tril(jnp.ones((T, T), bool))
        scores = jnp.where(causal[None, None], scores, -jnp.inf)
        attn = jax.nn.softmax(scores, axis=-1)
        ao = jnp.einsum('bhqk,bhkd->bhqd', attn, v).transpose(0, 2, 1, 3).reshape(B, T, C) @ wo.T
        ao = ao.at[:, :, :M].set(0.0)
        x = x + ao
        xf = _rms(x, n2_w).reshape(-1, C)
        N = xf.shape[0]
        logits = jnp.nan_to_num(xf @ gate_w.T)
        probs = jax.nn.softmax(logits, axis=-1)
        topv, topi = jax.lax.top_k(probs, K)
        topv = topv / (topv.sum(-1, keepdims=True) + 1e-08)
        wts = jnp.zeros((N, E), x.dtype).at[jnp.arange(N)[:, None], topi].add(topv)
        o0 = _gelu(xf @ e0_up.T) @ e0_down.T
        o1 = jax.nn.silu(xf @ e1_w1.T) * (xf @ e1_w2.T) @ e1_down.T
        o2 = _gelu(_gelu(_gelu(xf @ e2_l1.T) @ e2_l2.T) @ e2_l3.T) @ e2_l4.T
        o3 = _gelu(_gelu(xf @ e3_down.T) @ e3_up.T) @ e3_out.T
        moe = wts[:, 0:1] * o0 + wts[:, 1:2] * o1 + wts[:, 2:3] * o2 + wts[:, 3:4] * o3
        moe = moe.reshape(B, T, C).at[:, :, :M].set(0.0)
        return x + moe
    x = x + _L0_attn_ref(_layernorm(x, axis=-1), L0_attn_w1, L0_attn_b1, L0_attn_ww, L0_attn_bw, L0_attn_w2, L0_attn_b2, L0_attn_gamma, L0_attn_beta)
    x = x + _L0_xattn_ref(_layernorm(x, axis=-1), ctx_768, L0_xattn_g_x, L0_xattn_b_x, L0_xattn_g_c, L0_xattn_b_c, L0_xattn_Wq, L0_xattn_Wk, L0_xattn_Wv, L0_xattn_Wo)
    x = x + _L0_ffn_ref(_layernorm(x, axis=-1), L0_ffn_bn_gamma, L0_ffn_bn_beta, L0_ffn_w_q, L0_ffn_keys_p, L0_ffn_down, L0_ffn_up)
    x = x + _L1_attn_ref(_layernorm(x, axis=-1), L1_attn_w_ln_z, L1_attn_b_ln_z, L1_attn_w_dt, L1_attn_b_dt, L1_attn_w_y, L1_attn_b_y, L1_attn_w_yact, L1_attn_b_yact, L1_attn_h0, L1_attn_w_fc, L1_attn_b_fc, L1_attn_w_fcact, L1_attn_b_fcact, L1_attn_w_out, L1_attn_b_out, L1_attn_g_sio, L1_attn_g_ffn)
    x = x + _L1_xattn_ref(_layernorm(x, axis=-1), ctx_768, L1_xattn_q_w, L1_xattn_q_b, L1_xattn_kv_w, L1_xattn_kv_b, L1_xattn_proj_w, L1_xattn_proj_b)
    x = x + _L1_ffn_ref(_layernorm(x, axis=-1), L1_ffn_n1_w, L1_ffn_n2_w, L1_ffn_wq, L1_ffn_wk, L1_ffn_wv, L1_ffn_wo, L1_ffn_qn_w, L1_ffn_kn_w, L1_ffn_gate_w, L1_ffn_e0_up, L1_ffn_e0_down, L1_ffn_e1_w1, L1_ffn_e1_w2, L1_ffn_e1_down, L1_ffn_e2_l1, L1_ffn_e2_l2, L1_ffn_e2_l3, L1_ffn_e2_l4, L1_ffn_e3_down, L1_ffn_e3_up, L1_ffn_e3_out)
    return x

_drawn_inputs = setup_inputs


def setup_inputs(seed=0):
    import zlib

    import numpy as np

    out = dict(_drawn_inputs(seed))
    spreads = {'L0_attn_b1': (0.0, 0.8),
     'L0_attn_bw': (0.0, 0.8),
     'L0_attn_b2': (0.0, 0.1),
     'L0_attn_gamma': (1.0, 0.2),
     'L0_attn_beta': (0.0, 0.1),
     'L0_xattn_g_x': (1.0, 0.6),
     'L0_xattn_b_x': (0.0, 0.8),
     'L0_xattn_g_c': (1.0, 0.2),
     'L0_xattn_b_c': (0.0, 0.1),
     'L0_ffn_bn_gamma': (1.0, 0.6),
     'L0_ffn_bn_beta': (0.0, 0.8),
     'L1_attn_g_sio': (1.0, 0.6),
     'L1_attn_g_ffn': (1.0, 0.6),
     'L1_xattn_q_b': (0.0, 0.8),
     'L1_xattn_kv_b': (0.0, 0.1),
     'L1_xattn_proj_b': (0.0, 0.1),
     'L1_ffn_n1_w': (1.0, 0.6),
     'L1_ffn_n2_w': (1.0, 0.6),
     'L1_ffn_qn_w': (1.0, 0.6),
     'L1_ffn_kn_w': (1.0, 0.6)}
    factors = {'L0_ffn_w_q': 8.0,
     'L0_ffn_keys_p': 8.0,
     'L0_ffn_down': 8.0,
     'L0_ffn_up': 8.0,
     'L1_attn_w_ln_z': 8.0,
     'L1_attn_b_ln_z': 54.773,
     'L1_attn_w_dt': 8.0,
     'L1_attn_b_dt': 35.716,
     'L1_attn_b_y': 8.0,
     'L1_attn_b_yact': 8.0,
     'L1_attn_h0': 8.0,
     'L1_attn_b_fc': 8.0,
     'L1_attn_b_fcact': 8.0,
     'L1_attn_b_out': 8.0,
     'L1_ffn_wq': 8.0,
     'L1_ffn_wk': 8.0,
     'L1_ffn_wv': 7.139,
     'L1_ffn_wo': 7.044,
     'L1_ffn_gate_w': 8.0,
     'L1_ffn_e0_up': 8.0,
     'L1_ffn_e0_down': 8.0,
     'L1_ffn_e1_w1': 8.0,
     'L1_ffn_e1_w2': 8.0,
     'L1_ffn_e1_down': 8.0,
     'L1_ffn_e2_l1': 8.0,
     'L1_ffn_e2_l2': 8.0,
     'L1_ffn_e2_l3': 8.0,
     'L1_ffn_e2_l4': 8.0,
     'L1_ffn_e3_down': 8.0,
     'L1_ffn_e3_up': 8.0,
     'L1_ffn_e3_out': 8.0}
    for name, (base, spread) in spreads.items():
        noise = np.random.default_rng([zlib.crc32(name.encode()), seed]).standard_normal(out[name].shape)
        drawn = base * np.exp(spread * noise) if base else spread * noise
        out[name] = jnp.asarray(drawn.astype(out[name].dtype))
    for name, factor in factors.items():
        out[name] = (out[name] * factor).astype(out[name].dtype)
    return out
```

```python
from contextlib import ExitStack

import concourse.bass as bass
import numpy as np
from concourse import mybir
from concourse.alu_op_type import AluOpType as ALU

ACT = mybir.ActivationFunctionType
AX = mybir.AxisListType
F32 = mybir.dt.float32
U32 = mybir.dt.uint32

P = 128
BATCH, SEQ, DIM = 2, 512, 256
TOKENS = BATCH * SEQ
TILES = TOKENS // P
SEQ_TILES = SEQ // P
DC = DIM // P
KEYS, CTX = 1024, 192
CTX_TILES = BATCH * KEYS // P
CK = CTX // 2
BANK = 512
HEADS = 16

TAPS = 31
PK_HEADS, PK_DIM, PK_KEYS, TOP = 8, 128, 64, 8
EXPERTS = PK_KEYS * PK_KEYS
PICKS = PK_HEADS * TOP
FF, HID, GATES = 1024, 512, 4
MASKED = 64


class Names:

    def __init__(self, nc, ctx, stage):
        self.nc, self.ctx, self.stage = nc, ctx, stage

    def sb(self, name, shape, dtype=F32):
        return self.ctx.enter_context(self.nc.sbuf_tensor(f"{self.stage}_{name}", shape, dtype))

    def sem(self, name):
        return self.nc.alloc_semaphore(f"{self.stage}_{name}")


class Psum:

    def __init__(self, tensor):
        self.all = tensor
        self.banks = [tensor[:, n * BANK:(n + 1) * BANK] for n in range(8)]
        self.norm_sems = {}


def hold(dve, semaphore, value, scratch):
    dve.wait_ge(semaphore, value)
    dve.memset(scratch, 0.0)


class Counted:

    def __init__(self, semaphore):
        self.semaphore, self.base = semaphore, 0

    def wait(self, engine, value):
        engine.wait_ge(self.semaphore, self.base + value)

    def used(self, increments):
        self.base += increments


class Chain:

    def __init__(self, engine, semaphore, turn=0, per_turn=0):
        self.engine, self.semaphore, self.count = engine, semaphore, 0
        self.turn, self.per_turn = turn, per_turn

    def link(self, instruction, scratch=None):
        self.count += 1
        instruction.then_inc(self.semaphore, 1)
        value = self.turn * self.per_turn + self.count
        if scratch is not None:
            hold(self.engine, self.semaphore, value, scratch)
        else:
            self.engine.wait_ge(self.semaphore, value)

    def end(self):
        assert self.count == self.per_turn, (self.count, self.per_turn)


def load_row(eng, dst, row, semaphore):
    eng.dma_start(dst, row.partition_broadcast(P)).then_inc(semaphore, 16)


def by_tile(bank):
    return bank[:].rearrange("p (t d) -> p t d", d=DIM)


def over_tiles(row, tiles):
    return row[:].unsqueeze(1).to_broadcast([P, tiles, row.shape[1]])


def constants(nc, names):
    ident = names.sb("ident", [P, P])
    made = names.sem("ident_steps")
    with nc.Block() as block:

        @block.gpsimd
        def _(pool):
            chain = Chain(pool, made)
            chain.link(pool.memset(ident[:], 0.0))
            chain.link(pool.affine_select(out=ident[:], in_=ident[:], compare_op=ALU.not_equal, fill=1.0,
                                          base=0, pattern=[[-1, P]], channel_multiplier=1))
    return ident


NORM_SEMS = ("steps", "variance_ready", "root_ready", "rows_ready", "turned", "bank_read")


def norm(nc, stage, psum, ident, src, width, eps, centre=True, out_tok=None, out_feat=None,
         kw=P, gain=None, shift=None, loads=None, loaded=None, src_in=None, beside=None):
    bank = psum.banks
    tiles = src.shape[1]
    chunks = width // kw
    per_bank = BANK // P
    with ExitStack() as ctx:
        names = Names(nc, ctx, stage)
        stats = names.sb("stats", [P, tiles, 6])
        moments = names.sb("moments", [P, tiles, 2])
        power = names.sb("power", [P, tiles])
        spread = names.sb("spread", [P, tiles])
        root = names.sb("root", [P, tiles])
        rstd = names.sb("rstd", [P, tiles])
        normed = out_tok if out_tok is not None else names.sb("normed", [P, tiles, width])
        dve_steps, variance_ready, root_ready, rows_ready, turned, bank_read = (
            psum.norm_sems[n] for n in NORM_SEMS)
        groups = [(g, c) for g in range(tiles // per_bank) for c in range(chunks)]
        with nc.Block() as block:
            if loads is not None:
                @block.sync
                def _(sync):
                    loads(sync)

            @block.vector
            def _(dve):
                chain = Chain(dve, dve_steps.semaphore, dve_steps.base, 1)
                if src_in is not None:
                    dve.wait_ge(*src_in)
                for t in range(tiles):
                    last = dve.bn_stats(stats[:, t, :], src[:, t, :])
                chain.link(last)
                for t in range(tiles):
                    last = dve.bn_aggr(moments[:, t, :], stats[:, t, :])
                chain.link(last)
                if centre:
                    dve.tensor_scalar(spread[:], moments[:, :, 1], eps, None, ALU.add).then_inc(variance_ready.semaphore, 1)
                else:
                    chain.link(dve.tensor_tensor(power[:], moments[:, :, 0], moments[:, :, 0], ALU.mult))
                    dve.scalar_tensor_tensor(out=spread[:], in0=moments[:, :, 1], scalar=eps, in1=power[:],
                                             op0=ALU.add, op1=ALU.add).then_inc(variance_ready.semaphore, 1)
                root_ready.wait(dve, 1)
                chain.link(dve.reciprocal(rstd[:], root[:]))
                for t in range(tiles):
                    if centre:
                        dve.tensor_scalar(normed[:, t, :], src[:, t, :], moments[:, t, 0:1], rstd[:, t:t + 1],
                                          ALU.subtract, ALU.mult).then_inc(rows_ready.semaphore, 1)
                    else:
                        dve.tensor_scalar(normed[:, t, :], src[:, t, :], rstd[:, t:t + 1], None,
                                          ALU.mult).then_inc(rows_ready.semaphore, 1)

            @block.scalar
            def _(act):
                variance_ready.wait(act, 1)
                act.activation(root[:], spread[:], ACT.Sqrt).then_inc(root_ready.semaphore, 1)
                if beside is not None:
                    beside[1](act)
                if out_feat is None:
                    return
                if loaded is not None:
                    act.wait_ge(*loaded)
                for n, (g, c) in enumerate(groups):
                    dst = out_feat[:, c, g * BANK:(g + 1) * BANK]
                    turned.wait(act, n + 1)
                    if gain is None:
                        act.activation(dst, bank[n % 2][0:kw, :], ACT.Copy).then_inc(bank_read.semaphore, 1)
                    elif shift is None:
                        act.activation(dst, bank[n % 2][0:kw, :], ACT.Copy,
                                       scale=gain[:, c:c + 1]).then_inc(bank_read.semaphore, 1)
                    else:
                        act.activation(dst, bank[n % 2][0:kw, :], ACT.Identity, bias=shift[:, c:c + 1],
                                       scale=gain[:, c:c + 1]).then_inc(bank_read.semaphore, 1)

            if out_feat is not None or beside is not None:
                @block.tensor
                def _(pe):
                    if beside is not None:
                        beside[0](pe)
                    if out_feat is None:
                        return
                    for n, (g, c) in enumerate(groups):
                        if n >= 2:
                            bank_read.wait(pe, n - 1)
                        for k in range(per_bank):
                            t = g * per_bank + k
                            rows_ready.wait(pe, t + 1)
                            last = pe.transpose(bank[n % 2][0:kw, k * P:(k + 1) * P],
                                                normed[:, t, c * kw:(c + 1) * kw], ident[:])
                        last.then_inc(turned.semaphore, 1)

        dve_steps.used(3 if centre else 4)
        variance_ready.used(1)
        root_ready.used(1)
        rows_ready.used(tiles)
        if out_feat is not None:
            turned.used(len(groups))
            bank_read.used(len(groups))


def dynamic_conv(nc, dram, psum, ident, x):
    bank = psum.banks
    with ExitStack() as ctx:
        names = Names(nc, ctx, "conv")
        y = names.sb("y", [P, TILES, DIM])
        yt = names.sb("yt", [P, DC, TOKENS])
        w1 = names.sb("w1", [P, DC, DIM])
        w2 = names.sb("w2", [P, DC, DIM])
        ww = names.sb("ww", [P, DC, HEADS * TAPS])
        b1 = names.sb("b1", [P, DIM])
        b2 = names.sb("b2", [P, DIM])
        bw = names.sb("bw", [P, HEADS * TAPS])
        gamma = names.sb("gamma", [P, DIM])
        beta = names.sb("beta", [P, DIM])
        h = names.sb("h", [P, TILES, DIM])
        ht = names.sb("ht", [P, DC, TOKENS])
        logits = names.sb("logits", [P, 2, HEADS, TAPS])
        top = names.sb("top", [P, 2, HEADS])
        total = names.sb("total", [P, 2, HEADS])
        inverse = names.sb("inverse", [P, 2, HEADS])
        taps = names.sb("taps", [P, TILES, 2, HEADS])
        conv = names.sb("conv", [P, TILES, DIM])
        older = names.sb("older", [P, SEQ_TILES, DIM])
        convt = names.sb("convt", [P, DC, TOKENS])
        mixed = names.sb("mixed", [P, TILES, DIM])
        weights_in = names.sem("weights_in")
        dve_steps = names.sem("dve_steps")
        h_made = names.sem("h_made")
        h_ready = names.sem("h_ready")
        h_turned = names.sem("h_turned")
        ht_ready = names.sem("ht_ready")
        logits_made = names.sem("logits_made")
        shifted = names.sem("shifted")
        exped = names.sem("exped")
        conv_ready = names.sem("conv_ready")
        conv_turned = names.sem("conv_turned")
        convt_ready = names.sem("convt_ready")
        out_made = names.sem("out_made")
        mixed_ready = names.sem("mixed_ready")

        def loads(sync):
            sync.dma_start(w1[:], dram["L0_attn_w1"]).then_inc(weights_in, 16)
            sync.dma_start(ww[:], dram["L0_attn_ww"]).then_inc(weights_in, 16)
            sync.dma_start(w2[:], dram["L0_attn_w2"]).then_inc(weights_in, 16)
            for dst, name in ((b1, "b1"), (bw, "bw"), (b2, "b2"), (gamma, "gamma"), (beta, "beta")):
                load_row(sync, dst[:], dram[f"L0_attn_{name}"], weights_in)

        norm(nc, "conv_norm", psum, ident, x, DIM, 1e-5, out_tok=y, out_feat=yt, loads=loads)

        with nc.Block() as block:
            @block.tensor
            def _(pe):
                pe.wait_ge(weights_in, 16 * 8)
                for t in range(TILES):
                    pair = t // 2
                    if t % 2 == 0 and pair >= 2:
                        pe.wait_ge(h_ready, pair - 1)
                    for c in range(DC):
                        last = pe.matmul(bank[pair % 2][:, (t % 2) * DIM:(t % 2 + 1) * DIM],
                                         yt[:, c, t * P:(t + 1) * P], w1[:, c, :], start=c == 0, stop=c == DC - 1)
                    if t % 2:
                        last.then_inc(h_made, 1)
                for n in range(DC * 2):
                    g, c = n // DC, n % DC
                    if n >= 2:
                        pe.wait_ge(ht_ready, n - 1)
                    for k in range(4):
                        t = 4 * g + k
                        pe.wait_ge(h_ready, t // 2 + 1)
                        last = pe.transpose(bank[2 + n % 2][:, k * P:(k + 1) * P], h[:, t, c * P:(c + 1) * P], ident[:])
                    last.then_inc(h_turned, 1)
                for t in range(TILES):
                    pe.wait_ge(ht_ready, 2 * (t // 4) + 2)
                    if t >= 2:
                        pe.wait_ge(shifted, t - 1)
                    for c in range(DC):
                        last = pe.matmul(bank[4 + t % 2][:, 0:HEADS * TAPS], ht[:, c, t * P:(t + 1) * P], ww[:, c, :],
                                         start=c == 0, stop=c == DC - 1)
                    last.then_inc(logits_made, 1)
                for n in range(DC * 2):
                    g, c = n // DC, n % DC
                    if n >= 2:
                        pe.wait_ge(convt_ready, n - 1)
                    for k in range(4):
                        t = 4 * g + k
                        pe.wait_ge(conv_ready, t + 1)
                        last = pe.transpose(bank[2 + n % 2][:, k * P:(k + 1) * P], conv[:, t, c * P:(c + 1) * P],
                                            ident[:])
                    last.then_inc(conv_turned, 1)
                for t in range(TILES):
                    pair = t // 2
                    pe.wait_ge(convt_ready, 2 * (t // 4) + 2)
                    if t % 2 == 0 and pair >= 2:
                        pe.wait_ge(mixed_ready, pair - 1)
                    for c in range(DC):
                        last = pe.matmul(bank[pair % 2][:, (t % 2) * DIM:(t % 2 + 1) * DIM],
                                         convt[:, c, t * P:(t + 1) * P], w2[:, c, :], start=c == 0, stop=c == DC - 1)
                    if t % 2:
                        last.then_inc(out_made, 1)

            @block.scalar
            def _(act):
                for n in range(DC * 2):
                    g, c = n // DC, n % DC
                    act.wait_ge(h_turned, n + 1)
                    act.activation(ht[:, c, g * BANK:(g + 1) * BANK], bank[2 + n % 2][:], ACT.Copy).then_inc(ht_ready, 1)
                for t in range(TILES):
                    act.wait_ge(shifted, t + 1)
                    act.activation(logits[:, t % 2], logits[:, t % 2], ACT.Exp).then_inc(exped, 1)
                for n in range(DC * 2):
                    g, c = n // DC, n % DC
                    act.wait_ge(conv_turned, n + 1)
                    act.activation(convt[:, c, g * BANK:(g + 1) * BANK], bank[2 + n % 2][:],
                                   ACT.Copy).then_inc(convt_ready, 1)

            @block.vector
            def _(dve):
                chain = Chain(dve, dve_steps)
                dve.wait_ge(weights_in, 16 * 8)
                for pair in range(TILES // 2):
                    dve.wait_ge(h_made, pair + 1)
                    dve.tensor_tensor(h[:, 2 * pair:2 * pair + 2, :], by_tile(bank[pair % 2]), over_tiles(b1, 2),
                                      ALU.add).then_inc(h_ready, 1)

                def shift_logits(t):
                    rows = logits[:, t % 2]
                    dve.wait_ge(logits_made, t + 1)
                    chain.link(dve.tensor_tensor(rows.rearrange("p h k -> p (h k)"), bank[4 + t % 2][:, 0:HEADS * TAPS],
                                                 bw[:], ALU.add))
                    chain.link(dve.tensor_reduce(top[:, t % 2, :], rows, AX.X, ALU.max))
                    dve.tensor_tensor(rows, rows, top[:, t % 2, :].unsqueeze(2).to_broadcast([P, HEADS, TAPS]),
                                      ALU.subtract).then_inc(shifted, 1)

                def weigh(t):
                    rows = logits[:, t % 2]
                    dve.wait_ge(exped, t + 1)
                    chain.link(dve.tensor_reduce(total[:, t % 2, :], rows, AX.X, ALU.add))
                    chain.link(dve.reciprocal(inverse[:, t % 2, :], total[:, t % 2, :]))
                    for k in range(2):
                        last = dve.tensor_tensor(taps[:, t, k, :], rows[:, :, TAPS - 2 + k], inverse[:, t % 2, :],
                                                 ALU.mult)
                    chain.link(last)

                shift_logits(0)
                for t in range(TILES):
                    if t + 1 < TILES:
                        shift_logits(t + 1)
                    weigh(t)

                def by_head(a):
                    return a.rearrange("p (h r) -> p h r", h=HEADS)

                def weight(t, k):
                    return taps[:, t, k, :].unsqueeze(2).to_broadcast([P, HEADS, DIM // HEADS])

                for t in range(TILES):
                    own = dve.tensor_tensor(by_head(conv[:, t, :]), by_head(h[:, t, :]), weight(t, 1), ALU.mult)
                    if t < SEQ_TILES:
                        own.then_inc(conv_ready, 1)
                    else:
                        j = t - SEQ_TILES
                        chain.link(dve.tensor_tensor(by_head(older[:, j, :]), by_head(h[:, j, :]), weight(t, 0), ALU.mult))
                        dve.tensor_tensor(conv[:, t, :], conv[:, t, :], older[:, j, :], ALU.add).then_inc(conv_ready, 1)
                for pair in range(TILES // 2):
                    both = slice(2 * pair, 2 * pair + 2)
                    dve.wait_ge(out_made, pair + 1)
                    chain.link(dve.tensor_tensor(mixed[:, both, :], by_tile(bank[pair % 2]), over_tiles(b2, 2), ALU.add))
                    dve.tensor_tensor(mixed[:, both, :], mixed[:, both, :], y[:, both, :], ALU.add).then_inc(mixed_ready, 1)

        norm(nc, "conv_out", psum, ident, mixed, DIM, 1e-5, out_tok=conv)
        with nc.Block() as block:
            @block.vector
            def _(dve):
                steps = Chain(dve, names.sem("residual_steps"))
                for op, row in ((ALU.mult, gamma), (ALU.add, beta)):
                    steps.link(dve.tensor_tensor(conv[:], conv[:], over_tiles(row, TILES), op))
                steps.link(dve.tensor_tensor(x[:], x[:], conv[:], ALU.add))


F32R = mybir.dt.float32r
QUAD = 4
HEAD = DIM // HEADS
PARTS = 4 * HEAD
ROWS = P


def wait_from(engine, semaphore, value):
    if not isinstance(value, int) or value > 0:
        engine.wait_ge(semaphore, value)


class Fills:

    def __init__(self):
        self.done, self.turn, self.per_turn = 0, 0, 0

    def enter(self, turn, per_turn):
        self.first, self.turn, self.per_turn = self.done, turn, per_turn

    def leave(self, turns):
        assert self.done - self.first == self.per_turn and self.per_turn % 2 == 0
        self.done += (turns - 1) * self.per_turn
        self.turn = self.per_turn = 0

    def next(self):
        self.done += 1
        if self.per_turn:
            return (self.done - 1) % 2, self.turn * self.per_turn + self.done
        return (self.done - 1) % 2, self.done


class StreamedAttention:

    def __init__(self, nc, names, psum, ident, qh, ql, kh, kl, v, attended, keys, causal=False):
        self.nc, self.ident, self.psum, self.bank = nc, ident, psum, psum.banks
        self.qh, self.ql, self.kh, self.kl, self.v, self.attended = qh, ql, kh, kl, v, attended
        self.keys, self.causal = keys, causal
        self.key_tiles = keys // P
        self.units = BATCH * HEADS
        self.turns = self.units // QUAD
        if causal:
            self.pieces = [[(0, (tile + 1) * P)] for tile in range(SEQ_TILES)]
        else:
            self.pieces = [[(k, BANK) for k in range(0, keys, BANK)] for _ in range(SEQ_TILES)]
        self.per_unit = sum(len(p) for p in self.pieces)
        if causal:
            self.steps = [[(0, 0, 0), (1, P, BANK), (3, 3 * P, BANK + 3 * P)], [(2, 2 * P, 0)]]
        else:
            self.steps = [[(k, 0, 0), (k + 1, 0, BANK)] for k in range(0, self.key_tiles, 2)]
        self.n_steps = len(self.steps)
        self.k_fills = keys // BANK
        self.pairs = [psum.all[:, (2 + 2 * n) * BANK:(4 + 2 * n) * BANK] for n in range(2)]
        self.q_packed = names.sb("q_packed", [P, QUAD, SEQ_TILES, ROWS], F32R)
        self.k_packed = names.sb("k_packed", [P, QUAD, self.key_tiles, ROWS], F32R)
        self.v_packed = names.sb("v_packed", [P, QUAD, self.key_tiles, P // QUAD])
        self.qt = names.sb("qt", [ROWS, QUAD, SEQ], F32R)
        self.kt = names.sb("kt", [ROWS, QUAD, keys], F32R)
        self.ident_r = names.sb("ident_r", [P, P], F32R)
        halves = len(self.pieces[0])
        self.half_max = names.sb("half_max", [P, 2, SEQ_TILES, halves])
        self.shift = names.sb("shift", [P, 2, SEQ_TILES])
        self.shift_parts = names.sb("shift_parts", [P, 2, SEQ_TILES, 2], F32R)
        self.probs = names.sb("probs", [P, 4, 2 * BANK])
        self.outputs = names.sb("outputs", [P, SEQ])
        self.gathered = names.sb("gathered", [P, SEQ_TILES, HEAD + 1])
        self.inverse = names.sb("inverse", [P, SEQ_TILES])
        if causal:
            self.masks = names.sb("masks", [P, 2, P])
            self.masks_r = names.sb("masks_r", [P, 2, P], F32R)
        self.constants_ready = names.sem("constants_ready")
        self.rounded = names.sem("rounded")
        self.packed = names.sem("packed")
        self.values_packed = names.sem("values_packed")
        self.q_turned = names.sem("q_turned")
        self.k_turned = names.sem("k_turned")
        self.out_turned = names.sem("out_turned")
        self.q_taken = names.sem("q_taken")
        self.k_taken = names.sem("k_taken")
        self.out_taken = names.sem("out_taken")
        self.filled = names.sem("filled")
        self.emptied = names.sem("emptied")
        self.shift_steps = names.sem("shift_steps")
        self.shifted = names.sem("shifted")
        self.exped = names.sem("exped")
        self.valued = names.sem("valued")
        self.outputs_read = names.sem("outputs_read")
        self.inverted = names.sem("inverted")
        self.divided = names.sem("divided")
        self.shift_links = 2 if causal else 3

    def count(self, turn, slot, ahead, per_unit=1, more=0):
        return turn * (QUAD * per_unit) + ((slot + ahead) * per_unit + more)

    def exists(self, turn, slot, ahead):
        return not isinstance(turn, int) or 0 <= turn * QUAD + slot + ahead < self.units

    def walk(self, engine, slot, fills=None):
        for h in range(1, QUAD):
            slot(-1, h)
        for h in range(QUAD):
            slot(0, h)
        loops = self.turns - 2
        with engine.Fori(1, self.turns - 1) as turn:
            if fills is not None:
                fills.enter(turn - 1, QUAD * (self.per_unit + 1))
            for h in range(QUAD):
                slot(turn, h)
            if fills is not None:
                fills.leave(loops)
        for h in range(QUAD):
            slot(self.turns - 1, h)
        slot(self.turns, 0)

    def pool(self, pool):
        steps = self.constants_ready
        n = 0

        def step(instruction):
            nonlocal n
            n += 1
            instruction.then_inc(steps, 1)
            pool.wait_ge(steps, n)

        if self.causal:
            step(pool.memset(self.masks[:], 0.0))
            for side, sign in ((0, 1), (1, -1)):
                step(pool.affine_select(out=self.masks[:, side, :], in_=self.masks[:, side, :], compare_op=ALU.is_ge,
                                        fill=-1e38, base=0, pattern=[[-sign, P]], channel_multiplier=sign))
        step(pool.memset(self.q_packed[:].bitcast(F32), 0.0))
        step(pool.memset(self.v_packed[:], 0.0))
        step(pool.memset(self.v_packed[:, :, :, HEAD:HEAD + 1], 1.0))
        pool.wait_ge(self.rounded, 1)

        quads = self.turns // BATCH

        def rows(src, turn, h, tiles):
            return src[:, bass.ds(turn // quads * tiles, tiles), bass.ds(turn % quads * (QUAD * HEAD) + h * HEAD, HEAD)]

        def pack_operands(turn, h):
            wait_from(pool, self.k_turned, self.count(turn, h, 1 - QUAD, self.k_fills))
            ring = h
            for part, (q, k) in enumerate(((self.qh, self.kh), (self.ql, self.kl))):
                dst = self.q_packed[:, ring, :, part * 2 * HEAD:(part + 1) * 2 * HEAD]
                pool.tensor_copy(dst.rearrange("p t (a r) -> p t a r", r=HEAD),
                                 rows(q, turn, h, SEQ_TILES).unsqueeze(2).to_broadcast([P, SEQ_TILES, 2, HEAD]))
                dst = self.k_packed[:, ring, :, 0:PARTS].rearrange("p t (a b r) -> p t a b r", b=2, r=HEAD)
                last = pool.tensor_copy(dst[:, :, :, part, :], rows(k, turn, h, self.key_tiles).unsqueeze(2).to_broadcast(
                    [P, self.key_tiles, 2, HEAD]))
            last.then_inc(self.packed, 1)

        def pack_values(turn, h):
            if not isinstance(turn, int) or turn > 0:
                pool.wait_ge(self.valued, self.count(turn, h, -3, self.n_steps))
            pool.tensor_copy(self.v_packed[:, h, :, 0:HEAD], rows(self.v, turn, h, self.key_tiles)
                             ).then_inc(self.values_packed, 1)

        def pack_turn(turn):
            for h in range(QUAD):
                pack_operands(turn, h)
                if h >= 2:
                    pack_values(turn, h - 2)
                elif not isinstance(turn, int) or turn > 0:
                    pack_values(turn - 1, h + 2)

        pack_turn(0)
        pack_turn(1)
        with pool.Fori(2, self.turns) as turn:
            pack_turn(turn)
        for h in (2, 3):
            pack_values(self.turns - 1, h)

    def tensor(self, pe):
        fills = Fills()
        before = [None]

        def fill_last(emit, done, taken, value):
            if before[0] is not None:
                wait_from(pe, *before[0])
            emit(self.bank[7]).then_inc(done, 1)
            before[0] = (taken, value)

        def fill_first(emit):
            n, number = fills.next()
            wait_from(pe, self.emptied, number - 2)
            emit(self.bank[n]).then_inc(self.filled, 1)

        rows_at = {}

        def rows_fill(turn, h):
            if isinstance(turn, int) and turn * QUAD + h in rows_at:
                return rows_at[turn * QUAD + h]
            return fills.turn * fills.per_turn + fills.done - sum(len(p) for p in self.pieces[1:])

        def turn_four(packed, first):
            def emit(dst):
                for t in range(4):
                    last = pe.matmul(dst[0:ROWS, t * P:(t + 1) * P], packed[:, first + t, :], self.ident_r[:],
                                     start=True, stop=True)
                return last
            return emit

        def queries(turn, h):
            if self.exists(turn, h, 3):
                pe.wait_ge(self.packed, self.count(turn, h, 3, 1, 1))
                fill_last(turn_four(self.q_packed[:, (h + 3) % QUAD], 0), self.q_turned, self.q_taken,
                          self.count(turn, h, 3, 1, 1))

        def keys(turn, h, n):
            if n < self.k_fills and self.exists(turn, h, 3):
                fill_last(turn_four(self.k_packed[:, (h + 3) % QUAD], 4 * n), self.k_turned, self.k_taken,
                          self.count(turn, h, 3, self.k_fills, n + 1))

        def rows(turn, h):
            if not self.exists(turn, h, 1):
                return
            pe.wait_ge(self.shift_steps, self.count(turn, h, 1, self.shift_links, self.shift_links))

            def emit(dst):
                for t in range(SEQ_TILES):
                    last = pe.matmul(dst[PARTS:PARTS + 2, t * P:(t + 1) * P],
                                     self.shift_parts[:, (h + 1) % 2, t, :].bitcast(F32), self.ident[:],
                                     start=True, stop=True)
                return last

            fill_first(emit)
            if isinstance(turn, int):
                rows_at[turn * QUAD + h + 1] = fills.done

        def scores(turn, h, tile, piece):
            if piece >= len(self.pieces[tile]) or not self.exists(turn, h, 2):
                return
            buffer = (h + 2) % QUAD
            if tile == 0 and piece == 0:
                pe.wait_ge(self.k_taken, self.count(turn, h, 2, self.k_fills, self.k_fills))
            k0, width = self.pieces[tile][piece]

            def emit(dst):
                last = pe.matmul(dst[:, 0:width], self.qt[:, buffer, tile * P:(tile + 1) * P],
                                 self.kt[:, buffer, k0:k0 + width], start=True, stop=not self.causal,
                                 skip_group_check=self.causal)
                if self.causal:
                    last = pe.matmul(dst[:, width - P:width], self.ident_r[:], self.masks_r[:, 0, :], start=False,
                                     stop=True, skip_group_check=True)
                return last

            fill_first(emit)

        def shifted(turn, h, j):
            if not self.exists(turn, h, 0):
                return
            if j == 0:
                pe.wait_ge(self.emptied, rows_fill(turn, h))
            wait_from(pe, self.exped, self.count(turn, h, 0, self.n_steps, j - 1))
            for tile, q0, at in self.steps[j]:
                bank = self.pairs[j % 2][:, at:at + SEQ - q0]
                last = pe.matmul(bank, self.kt[:, h, tile * P:(tile + 1) * P], self.qt[:, h, q0:SEQ], start=True,
                                 stop=not self.causal, skip_group_check=self.causal)
                if self.causal:
                    last = pe.matmul(self.pairs[j % 2][:, at:at + P], self.ident_r[:], self.masks_r[:, 1, :],
                                     start=False, stop=True, skip_group_check=True)
            last.then_inc(self.shifted, 1)

        def values(turn, h, j):
            ahead, step = divmod(j - 2, self.n_steps)
            if not self.exists(turn, h, ahead):
                return
            head = (h + ahead) % QUAD
            if step == 0:
                pe.wait_ge(self.values_packed, self.count(turn, h, ahead, 1, 1))
                wait_from(pe, self.outputs_read, self.count(turn, h, ahead))
            pe.wait_ge(self.exped, self.count(turn, h, ahead, self.n_steps, step + 1))
            for tile, q0, at in self.steps[step]:
                o = slice(tile % 4 * P // 4, (tile % 4 + 1) * P // 4)
                last = pe.matmul(self.bank[6][o, q0:SEQ], self.v_packed[:, head, tile, :],
                                 self.probs[:, self.ring(head, step), at:at + SEQ - q0],
                                 start=tile < 4, stop=tile >= self.key_tiles - 4, skip_group_check=True)
            last.then_inc(self.valued, 1)

        def unit_outputs(turn, h):
            if not self.exists(turn, h, -1):
                return
            pe.wait_ge(self.outputs_read, self.count(turn, h, 0))

            def emit(dst):
                for t in range(SEQ_TILES):
                    last = pe.transpose(dst[:, t * P:(t + 1) * P], self.outputs[:, t * P:(t + 1) * P], self.ident[:])
                return last

            fill_last(emit, self.out_turned, self.out_taken, self.count(turn, h, 0))

        def slot(turn, h):
            if h == 0 and not isinstance(turn, int):
                before[0] = (self.out_taken, self.count(turn, h, -1))
            for j in range(4):
                if j < self.n_steps:
                    shifted(turn, h, j)
                if j == 1:
                    rows(turn, h)
                scores(turn, h, j, 0)
                if j == 3:
                    unit_outputs(turn, h)
                if j == 0:
                    queries(turn, h)
                if j in (1, 2):
                    keys(turn, h, j - 1)
                if j < self.n_steps:
                    values(turn, h, j)
                scores(turn, h, j, 1)

        pe.wait_ge(self.rounded, 1)
        self.walk(pe, slot, fills)

    def ring(self, head, step):
        return (head * self.n_steps + step) % 4

    def scalar(self, act):
        def take(dst, done, taken, value):
            act.wait_ge(done, value)
            act.activation(dst, self.bank[7][0:ROWS, :], ACT.Copy).then_inc(taken, 1)

        def slot(turn, h):
            for j in range(4):
                if j < self.n_steps and self.exists(turn, h, 0):
                    width = sum(SEQ - q0 for _, q0, _ in self.steps[j])
                    act.wait_ge(self.shifted, self.count(turn, h, 0, self.n_steps, j + 1))
                    wait_from(act, self.valued, self.count(turn, h, 0, self.n_steps, j - 3))
                    act.activation(self.probs[:, self.ring(h, j), 0:width], self.pairs[j % 2][:, 0:width],
                                   ACT.Exp).then_inc(self.exped, 1)
                buffer = (h + 3) % QUAD
                if j == 0 and self.exists(turn, h, 3):
                    take(self.qt[:, buffer, :], self.q_turned, self.q_taken, self.count(turn, h, 3, 1, 1))
                if 0 <= j - 1 < self.k_fills and self.exists(turn, h, 3):
                    take(self.kt[:, buffer, (j - 1) * BANK:j * BANK], self.k_turned, self.k_taken,
                         self.count(turn, h, 3, self.k_fills, j))
                if j == 1 and self.exists(turn, h, -1):
                    act.wait_ge(self.valued, self.count(turn, h, 0, self.n_steps))
                    act.activation(self.outputs[:], self.bank[6][:], ACT.Copy).then_inc(self.outputs_read, 1)

        self.walk(act, slot)

    def vector(self, dve):
        fills = Fills()

        def filled():
            n, number = fills.next()
            dve.wait_ge(self.filled, number)
            return self.bank[n]

        def wait_emptied():
            dve.wait_ge(self.emptied, fills.turn * fills.per_turn + fills.done)

        def maxima(turn, h, tile, piece):
            if piece >= len(self.pieces[tile]) or not self.exists(turn, h, 2):
                return
            ring = (h + 2) % 2
            width = self.pieces[tile][piece][1]
            if self.causal:
                dst = self.shift[:, ring, tile:tile + 1]
            else:
                dst = self.half_max[:, ring, tile, piece:piece + 1]
            dve.tensor_reduce(dst, filled()[:, 0:width], AX.X, ALU.max, negate=self.causal).then_inc(self.emptied, 1)

        def shift_part(turn, h, part):
            if not self.exists(turn, h, 2):
                return
            ring = (h + 2) % 2
            shift, high, low = self.shift[:, ring, :], self.shift_parts[:, ring, :, 0], self.shift_parts[:, ring, :, 1]
            if part == 0:
                wait_emptied()
                if not self.causal:
                    dve.tensor_reduce(shift, self.half_max[:, ring], AX.X, ALU.max, negate=True
                                      ).then_inc(self.shift_steps, 1)
                return
            if part == 2 or not self.causal:
                dve.wait_ge(self.shift_steps, self.count(turn, h, 2, self.shift_links, self.shift_links - 3 + part))
            if part == 1:
                dve.tensor_copy(high, shift).then_inc(self.shift_steps, 1)
            else:
                dve.tensor_tensor(low, shift, high.bitcast(F32), ALU.subtract).then_inc(self.shift_steps, 1)

        def outputs(turn, h, part):
            if not self.exists(turn, h, -1):
                return
            if part == 0:
                dve.wait_ge(self.out_turned, self.count(turn, h, 0))
                groups = self.bank[7].rearrange("p (t g r) -> p t r g", g=4, r=P // 4)[:, :, 0:HEAD + 1, :]
                wait_from(dve, self.divided, self.count(turn, h, -1))
                dve.tensor_reduce(self.gathered[:], groups, AX.X, ALU.add).then_inc(self.out_taken, 1)
            elif part == 1:
                dve.wait_ge(self.out_taken, self.count(turn, h, 0))
                dve.reciprocal(self.inverse[:], self.gathered[:, :, HEAD]).then_inc(self.inverted, 1)
            else:
                dve.wait_ge(self.inverted, self.count(turn, h, 0))
                quads = self.turns // BATCH
                its_turn, head = (turn, h - 1) if h else (turn - 1, QUAD - 1)
                dst = self.attended[:, bass.ds(its_turn // quads * SEQ_TILES, SEQ_TILES),
                                    bass.ds(its_turn % quads * (QUAD * HEAD) + head * HEAD, HEAD)]
                dve.tensor_tensor(dst, self.gathered[:, :, 0:HEAD],
                                  self.inverse[:].unsqueeze(2).to_broadcast([P, SEQ_TILES, HEAD]), ALU.mult
                                  ).then_inc(self.divided, 1)

        def slot(turn, h):
            for j in range(3):
                if j == 1 and self.exists(turn, h, 1):
                    dve.tensor_copy(self.qt[PARTS:PARTS + 2, (h + 1) % QUAD, :],
                                    filled()[PARTS:PARTS + 2, :]).then_inc(self.emptied, 1)
                for piece in range(2):
                    maxima(turn, h, j, piece)
            maxima(turn, h, 3, 0)
            outputs(turn, h, 0)
            maxima(turn, h, 3, 1)
            outputs(turn, h, 1)
            shift_part(turn, h, 0)
            outputs(turn, h, 2)
            shift_part(turn, h, 1)
            shift_part(turn, h, 2)

        dve.memset(self.k_packed[:].bitcast(F32), 1.0)
        if self.causal:
            dve.wait_ge(self.constants_ready, 3)
            dve.tensor_copy(self.masks_r[:], self.masks[:])
            dve.memset(self.bank[6], 0.0)
        dve.tensor_copy(self.ident_r[:], self.ident[:]).then_inc(self.rounded, 1)
        self.walk(dve, slot, fills)

    def run(self):
        with self.nc.Block() as block:
            @block.gpsimd
            def _(pool):
                self.pool(pool)

            @block.tensor
            def _(pe):
                self.tensor(pe)

            @block.scalar
            def _(act):
                self.scalar(act)

            @block.vector
            def _(dve):
                self.vector(dve)


def project(nc, names, psum, ident, attended, w, w_in, acc, add_from=0, load=None):
    bank = psum.banks
    chunks = w.shape[1]
    turned = names.sb("attended_t", [P, chunks, TOKENS])
    made, taken, projected = (names.sem(f"project_{n}") for n in ("made", "taken", "projected"))
    with nc.Block() as block:
        if load is not None:
            @block.sync
            def _(sync):
                sync.dma_start(w[:], load).then_inc(w_in[0], 16)

        @block.tensor
        def _(pe):
            for n in range(BATCH * chunks):
                g, c = divmod(n, chunks)
                if n >= 4:
                    pe.wait_ge(taken, n - 3)
                for k in range(4):
                    last = pe.transpose(bank[n % 4][:, k * P:(k + 1) * P], attended[4 * g + k][:, c * P:(c + 1) * P],
                                        ident[:])
                last.then_inc(made, 1)
            pe.wait_ge(w_in[0], w_in[1])
            for t in range(TILES):
                pe.wait_ge(taken, (t // 4 + 1) * chunks)
                for c in range(chunks):
                    last = pe.matmul(bank[4 + t // 2][:, (t % 2) * DIM:(t % 2 + 1) * DIM],
                                     turned[:, c, t * P:(t + 1) * P], w[:, c, :], start=c == 0, stop=c == chunks - 1)
                if t % 2:
                    last.then_inc(projected, 1)

        @block.scalar
        def _(act):
            for n in range(BATCH * chunks):
                g, c = divmod(n, chunks)
                act.wait_ge(made, n + 1)
                act.activation(turned[:, c, g * BANK:(g + 1) * BANK], bank[n % 4], ACT.Copy).then_inc(taken, 1)

        @block.vector
        def _(dve):
            for pair in range(TILES // 2):
                dve.wait_ge(projected, pair + 1)
                rows = acc[:, 2 * pair:2 * pair + 2, add_from:]
                dve.tensor_tensor(rows, rows, by_tile(bank[4 + pair])[:, :, add_from:], ALU.add)


WIDE = 64


class WideAttention(StreamedAttention):

    def __init__(self, nc, names, psum, ident, z, c, v, dram):
        self.nc, self.ident, self.psum, self.bank = nc, ident, psum, psum.banks
        self.z, self.c, self.v, self.dram = z, c, v, dram
        self.keys, self.key_tiles = KEYS, KEYS // P
        self.units = BATCH * HEADS
        self.turns = self.units // QUAD
        self.pieces = [[(k, BANK) for k in range(0, KEYS, BANK)] for _ in range(SEQ_TILES)]
        self.per_unit = sum(len(p) for p in self.pieces)
        self.n_steps = self.key_tiles // 2
        self.k_fills = KEYS // BANK
        self.pairs = [psum.all[:, (2 + 2 * n) * BANK:(4 + 2 * n) * BANK] for n in range(2)]
        self.w = {"q": names.sb("wq", [P, 2, DC, WIDE]), "k": names.sb("wk", [CK, 2, 2, WIDE])}
        self.q_high = names.sb("q_high", [P, QUAD, SEQ], F32R)
        self.q_low = names.sb("q_low", [P, QUAD, SEQ], F32R)
        self.k_both = names.sb("k_both", [P, QUAD, KEYS], F32R)
        self.k_ones = names.sb("k_ones", [P, QUAD, KEYS], F32R)
        self.values = names.sb("values", [P, 2, self.key_tiles, WIDE])
        self.ones = names.sb("ones", [P, 1])
        self.gather = names.sb("gather", [P, WIDE])
        self.crossed = names.sb("crossed", [P, BANK])
        self.joined = names.sb("joined", [P, BANK])
        self.half_max = names.sb("half_max", [P, 2, SEQ_TILES, 2])
        self.shift = names.sb("shift", [P, 2, SEQ_TILES])
        self.shift_parts = names.sb("shift_parts", [P, 2, SEQ_TILES, 2], F32R)
        self.probs = names.sb("probs", [P, 4, 2 * BANK])
        self.prob_sums = names.sb("prob_sums", [P, 2 * BANK])
        self.totals = names.sb("totals", [P, BANK])
        self.outputs = names.sb("outputs", [P, SEQ])
        self.inverse = names.sb("inverse", [P, SEQ_TILES])
        self.constants_ready = names.sem("constants_ready")
        self.weights_in = [names.sem(f"weights_{n}_in") for n in range(2)]
        self.q_made = names.sem("q_made")
        self.k_made = names.sem("k_made")
        self.out_turned = names.sem("out_turned")
        self.crossed_ready = names.sem("crossed_ready")
        self.joined_ready = names.sem("joined_ready")
        self.q_high_ready = names.sem("q_high_ready")
        self.k_high_ready = names.sem("k_high_ready")
        self.q_taken = names.sem("q_taken")
        self.k_taken = names.sem("k_taken")
        self.values_packed = names.sem("values_packed")
        self.out_taken = names.sem("out_taken")
        self.k_copied = names.sem("k_copied")
        self.summed = names.sem("summed")
        self.gathered = names.sem("gathered")
        self.filled = names.sem("filled")
        self.emptied = names.sem("emptied")
        self.shift_steps = names.sem("shift_steps")
        self.shifted = names.sem("shifted")
        self.exped = names.sem("exped")
        self.valued = names.sem("valued")
        self.outputs_read = names.sem("outputs_read")
        self.inverted = names.sem("inverted")
        self.shift_links = 3

    def sync(self, sync):
        def load(head, slot):
            for kind, name in (("q", "Wq"), ("k", "Wk")):
                sync.dma_start(self.w[kind][:, slot], self.dram[f"L0_xattn_{name}"][head]).then_inc(
                    self.weights_in[slot], 16)
        load(0, 0)
        load(1, 1)
        with sync.Fori(1, self.turns) as turn:
            for slot in range(2):
                sync.wait_ge(self.k_made, self.count(turn, 2 * slot, 2 - QUAD, self.k_fills))
                load(turn * 2 + slot, slot)

    def pool(self, pool):
        for n, (dst, value) in enumerate(((self.k_ones[WIDE:, :, :].bitcast(F32), 1.0),
                                          (self.q_low[WIDE:, :, :].bitcast(F32), 0.0), (self.ones[:], 1.0))):
            pool.memset(dst, value).then_inc(self.constants_ready, 1)
            pool.wait_ge(self.constants_ready, n + 1)

        def copy(dst, src):
            one = self.ones[0:src.shape[0], 0:1]
            while len(one.shape) < len(src.shape):
                one = one.unsqueeze(1)
            return pool.tensor_tensor(dst, src, one.to_broadcast(list(src.shape)), ALU.mult)

        def copy_keys(turn, h, n):
            if not self.exists(turn, h, 3):
                return
            pool.wait_ge(self.k_high_ready, self.count(turn, h, 3, self.k_fills, n + 1))
            cols = slice(n * BANK, (n + 1) * BANK)
            copy(self.k_ones[0:WIDE, (h + 3) % QUAD, cols], self.k_both[0:WIDE, (h + 3) % QUAD, cols].bitcast(F32)
                 ).then_inc(self.k_copied, 1)

        def pack_values(turn, h):
            if not self.exists(turn, h, 0):
                return
            b = h % 2
            wait_from(pool, self.valued, self.count(turn, h, -1, self.n_steps))
            rows = self.v[:, b * self.key_tiles:(b + 1) * self.key_tiles, bass.ds(turn * P + h // 2 * WIDE, WIDE)]
            pool.tensor_copy(self.values[:, h % 2], rows).then_inc(self.values_packed, 1)

        def add_probs(turn, h, step):
            if not self.exists(turn, h, 0):
                return
            n_sums = self.n_steps
            pool.wait_ge(self.exped, self.count(turn, h, 0, self.n_steps, step + 1))
            sums = self.prob_sums[:]
            if step == 1:
                wait_from(pool, self.summed, self.count(turn, h, 0, n_sums))
                before = self.probs[:, 0, :]
            else:
                before = sums
                pool.wait_ge(self.summed, self.count(turn, h, 0, n_sums, step - 1))
            pool.tensor_tensor(sums, before, self.probs[:, step, :], ALU.add).then_inc(self.summed, 1)
            if step == self.n_steps - 1:
                pool.wait_ge(self.summed, self.count(turn, h, 0, n_sums, step))
                wait_from(pool, self.out_turned, self.count(turn, h, 0))
                pool.tensor_tensor(self.totals[:], sums[:, 0:BANK], sums[:, BANK:], ALU.add).then_inc(self.summed, 1)

        def slot(turn, h):
            pack_values(turn, h)
            add_probs(turn, h, 1)
            copy_keys(turn, h, 0)
            add_probs(turn, h, 2)
            copy_keys(turn, h, 1)
            add_probs(turn, h, 3)

        self.walk(pool, slot)

    def tensor(self, pe):
        fills = Fills()
        before = [None]

        def fill_last(emit, done, taken, value):
            if before[0] is not None:
                wait_from(pe, *before[0])
            emit(self.bank[7]).then_inc(done, 1)
            before[0] = (taken, value)

        def fill_first(emit):
            n, number = fills.next()
            wait_from(pe, self.emptied, number - 2)
            emit(self.bank[n]).then_inc(self.filled, 1)

        rows_at = {}

        def rows_fill(turn, h):
            if isinstance(turn, int) and turn * QUAD + h in rows_at:
                return rows_at[turn * QUAD + h]
            return fills.turn * fills.per_turn + fills.done - sum(len(p) for p in self.pieces[1:])

        def project(turn, h, kind, n=0):
            if not self.exists(turn, h, 3):
                return
            slot, b = (h + 3) % QUAD // 2, (h + 3) % 2
            w = self.w[kind]

            def by_feature(x, first):
                def emit(dst):
                    for c in range(2):
                        last = pe.matmul(dst[c * WIDE:(c + 1) * WIDE, :], w[:, slot, c, :],
                                         x[:, c, first:first + BANK], start=True, stop=True, skip_group_check=True)
                    return last
                return emit

            if kind == "q":
                pe.wait_ge(self.weights_in[slot], (turn + (h + 3) // QUAD) * 32 + 32)
                fill_last(by_feature(self.z, b * SEQ), self.q_made, self.joined_ready, self.count(turn, h, 3, 3, 1))
            else:
                fill_last(by_feature(self.c, b * KEYS + n * BANK), self.k_made, self.joined_ready,
                          self.count(turn, h, 3, 3, n + 2))

        def rows(turn, h):
            if not self.exists(turn, h, 1):
                return
            pe.wait_ge(self.shift_steps, self.count(turn, h, 1, self.shift_links, self.shift_links))

            def emit(dst):
                for t in range(SEQ_TILES):
                    last = pe.matmul(dst[WIDE:WIDE + 2, t * P:(t + 1) * P],
                                     self.shift_parts[:, (h + 1) % 2, t, :].bitcast(F32), self.ident[:],
                                     start=True, stop=True)
                return last

            fill_first(emit)
            if isinstance(turn, int):
                rows_at[turn * QUAD + h + 1] = fills.done

        def scores(turn, h, tile, piece):
            if not self.exists(turn, h, 2):
                return
            buffer = (h + 2) % QUAD
            if tile == 0 and piece == 0:
                pe.wait_ge(self.k_taken, self.count(turn, h, 2, self.k_fills, self.k_fills))
                pe.wait_ge(self.k_copied, self.count(turn, h, 2, self.k_fills, self.k_fills))
            k0, width = self.pieces[tile][piece]
            q = slice(tile * P, (tile + 1) * P)

            def emit(dst):
                pe.matmul(dst, self.q_high[:, buffer, q], self.k_both[:, buffer, k0:k0 + width], start=True, stop=False)
                return pe.matmul(dst, self.q_low[0:WIDE, buffer, q], self.k_ones[0:WIDE, buffer, k0:k0 + width],
                                 start=False, stop=True)

            fill_first(emit)

        def shifted(turn, h, j):
            if not self.exists(turn, h, 0):
                return
            if j == 0:
                pe.wait_ge(self.emptied, rows_fill(turn, h))
            wait_from(pe, self.exped, self.count(turn, h, 0, self.n_steps, j - 1))
            for half in range(2):
                k = slice((2 * j + half) * P, (2 * j + half + 1) * P)
                bank = self.bank[2 + 2 * (j % 2) + half]
                pe.matmul(bank, self.k_both[:, h, k], self.q_high[:, h, :], start=True, stop=False)
                last = pe.matmul(bank, self.k_ones[:, h, k], self.q_low[:, h, :], start=False, stop=True)
            last.then_inc(self.shifted, 1)

        def values(turn, h, j):
            ahead, step = divmod(j - 2, self.n_steps)
            if not self.exists(turn, h, ahead):
                return
            buffer = (h + ahead) % 2
            if step == 0:
                pe.wait_ge(self.values_packed, self.count(turn, h, ahead, 1, 1))
                wait_from(pe, self.outputs_read, self.count(turn, h, ahead))
            pe.wait_ge(self.exped, self.count(turn, h, ahead, self.n_steps, step + 1))
            for half in range(2):
                tile = 2 * step + half
                last = pe.matmul(self.bank[6][half * WIDE:(half + 1) * WIDE, :], self.values[:, buffer, tile, :],
                                 self.probs[:, step, half * BANK:(half + 1) * BANK], start=step == 0,
                                 stop=step == self.n_steps - 1, skip_group_check=True)
            last.then_inc(self.valued, 1)

        def unit_outputs(turn, h):
            if not self.exists(turn, h, -1):
                return
            if isinstance(turn, int) and turn * QUAD + h == 1:
                pe.wait_ge(self.gathered, 1)
            pe.wait_ge(self.outputs_read, self.count(turn, h, 0))
            pe.wait_ge(self.summed, self.count(turn, h, 0, self.n_steps))

            def emit(dst):
                for t in range(SEQ_TILES):
                    pe.matmul(dst[:, t * P:t * P + WIDE], self.outputs[:, t * P:(t + 1) * P], self.gather[:],
                              start=True, stop=True, skip_group_check=True)
                    last = pe.matmul(dst[:, t * P + WIDE:t * P + WIDE + 1], self.totals[:, t * P:(t + 1) * P],
                                     self.ones[:], start=True, stop=True, skip_group_check=True)
                return last

            fill_last(emit, self.out_turned, self.out_taken, self.count(turn, h, 0))

        def slot(turn, h):
            if h == 0 and not isinstance(turn, int):
                before[0] = (self.out_taken, self.count(turn, h, -1))
            for j in range(4):
                shifted(turn, h, j)
                if j == 1:
                    rows(turn, h)
                if j == 0:
                    project(turn, h, "q")
                scores(turn, h, j, 0)
                if j == 1:
                    project(turn, h, "k", 0)
                values(turn, h, j)
                if j == 2:
                    project(turn, h, "k", 1)
                if j == 3:
                    unit_outputs(turn, h)
                scores(turn, h, j, 1)

        self.walk(pe, slot, fills)

    def scalar(self, act):
        scale = WIDE ** -0.5

        def cross(turn, h, n):
            if not self.exists(turn, h, 3):
                return
            if n == 0:
                act.wait_ge(self.q_made, self.count(turn, h, 3, 1, 1))
            else:
                act.wait_ge(self.k_made, self.count(turn, h, 3, self.k_fills, n))
            wait_from(act, self.joined_ready, self.count(turn, h, 3, 3, n))
            act.activation(self.crossed[0:WIDE, :], self.bank[7][WIDE:, :], ACT.Copy)
            act.activation(self.crossed[WIDE:, :], self.bank[7][0:WIDE, :], ACT.Copy).then_inc(self.crossed_ready, 1)

        def high_parts(turn, h, n):
            if not self.exists(turn, h, 3):
                return
            buffer = (h + 3) % QUAD
            act.wait_ge(self.joined_ready, self.count(turn, h, 3, 3, n + 1))
            if n == 0:
                act.activation(self.q_high[:, buffer, :], self.joined[:], ACT.Copy, scale=scale).then_inc(self.q_high_ready, 1)
            else:
                act.activation(self.k_both[:, buffer, (n - 1) * BANK:n * BANK], self.joined[:], ACT.Copy
                               ).then_inc(self.k_high_ready, 1)

        def slot(turn, h):
            for j in range(4):
                if j == 3:
                    high_parts(turn, h, 2)
                if self.exists(turn, h, 0):
                    act.wait_ge(self.shifted, self.count(turn, h, 0, self.n_steps, j + 1))
                    wait_from(act, self.valued, self.count(turn, h, 0, self.n_steps, j - 3))
                    wait_from(act, self.summed, self.count(turn, h, -1, self.n_steps, max(j, 1)))
                    act.activation(self.probs[:, j, :], self.pairs[j % 2], ACT.Exp).then_inc(self.exped, 1)
                if j in (1, 2):
                    high_parts(turn, h, j - 1)
                if h >= 0 and j == 1 and self.exists(turn, h, -1):
                    act.wait_ge(self.valued, self.count(turn, h, 0, self.n_steps))
                    act.activation(self.outputs[:], self.bank[6], ACT.Copy).then_inc(self.outputs_read, 1)
                if j < 3:
                    cross(turn, h, j)

        self.walk(act, slot)

    def vector(self, dve):
        fills = Fills()
        scale = WIDE ** -0.5

        def filled():
            n, number = fills.next()
            dve.wait_ge(self.filled, number)
            return self.bank[n]

        def maxima(turn, h, tile, piece):
            if not self.exists(turn, h, 2):
                return
            ring = (h + 2) % 2
            dve.tensor_reduce(self.half_max[:, ring, tile, piece:piece + 1], filled(), AX.X, ALU.max
                              ).then_inc(self.emptied, 1)
            if tile < SEQ_TILES - 1 or piece == 0:
                return
            dve.wait_ge(self.emptied, fills.turn * fills.per_turn + fills.done)
            dve.tensor_reduce(self.shift[:, ring, :], self.half_max[:, ring], AX.X, ALU.max,
                              negate=True).then_inc(self.shift_steps, 1)
            dve.wait_ge(self.shift_steps, self.count(turn, h, 2, self.shift_links, 1))
            high, low = self.shift_parts[:, ring, :, 0], self.shift_parts[:, ring, :, 1]
            dve.tensor_copy(high, self.shift[:, ring, :]).then_inc(self.shift_steps, 1)
            dve.wait_ge(self.shift_steps, self.count(turn, h, 2, self.shift_links, 2))
            dve.tensor_tensor(low, self.shift[:, ring, :], high.bitcast(F32), ALU.subtract).then_inc(self.shift_steps, 1)

        def join(turn, h, n):
            if not self.exists(turn, h, 3):
                return
            dve.wait_ge(self.crossed_ready, self.count(turn, h, 3, 3, n + 1))
            if n == 1:
                dve.wait_ge(self.q_taken, self.count(turn, h, 3, 1, 1))
            else:
                wait_from(dve, self.k_taken, self.count(turn, h, 3, self.k_fills, n // 2))
            dve.tensor_tensor(self.joined[:], self.bank[7], self.crossed[:], ALU.add).then_inc(self.joined_ready, 1)

        def low_parts(turn, h, kind, n=0):
            if not self.exists(turn, h, 3):
                return
            buffer = (h + 3) % QUAD
            if kind == "q":
                dve.wait_ge(self.q_high_ready, self.count(turn, h, 3, 1, 1))
                dve.scalar_tensor_tensor(out=self.q_low[0:WIDE, buffer, :], in0=self.joined[0:WIDE, :], scalar=scale,
                                         in1=self.q_high[0:WIDE, buffer, :].bitcast(F32), op0=ALU.mult,
                                         op1=ALU.subtract).then_inc(self.q_taken, 1)
            else:
                dve.wait_ge(self.k_high_ready, self.count(turn, h, 3, self.k_fills, n + 1))
                half = self.k_both[WIDE:, buffer, n * BANK:(n + 1) * BANK]
                dve.tensor_tensor(half, self.joined[WIDE:, :], half.bitcast(F32), ALU.subtract).then_inc(self.k_taken, 1)

        def unit_outputs(turn, h):
            if not self.exists(turn, h, -1):
                return
            dve.wait_ge(self.out_turned, self.count(turn, h, 0))
            turned = self.bank[7].rearrange("p (t r) -> p t r", r=P)
            dve.reciprocal(self.inverse[:], turned[:, :, WIDE]).then_inc(self.inverted, 1)
            dve.wait_ge(self.inverted, self.count(turn, h, 0))
            head = turn * 2 + (h - 1) // 2
            b = (h - 1) % 2
            first = b * self.key_tiles
            dst = self.v[:, first:first + SEQ_TILES, bass.ds(head * WIDE, WIDE)]
            dve.tensor_tensor(dst, turned[:, :, 0:WIDE], self.inverse[:].unsqueeze(2).to_broadcast(
                [P, SEQ_TILES, WIDE]), ALU.mult).then_inc(self.out_taken, 1)

        def slot(turn, h):
            for j in range(4):
                if j == 1 and self.exists(turn, h, 1):
                    dve.tensor_copy(self.q_low[WIDE:WIDE + 2, (h + 1) % QUAD, :], filled()[WIDE:WIDE + 2, :]
                                    ).then_inc(self.emptied, 1)
                maxima(turn, h, j, 0)
                if j == 0:
                    join(turn, h, 0)
                if j == 1:
                    low_parts(turn, h, "q")
                    join(turn, h, 1)
                if j == 2:
                    low_parts(turn, h, "k", 0)
                    join(turn, h, 2)
                if j == 3:
                    low_parts(turn, h, "k", 1)
                    unit_outputs(turn, h)
                maxima(turn, h, j, 1)

        dve.tensor_reduce(self.gather[:], self.ident[:].rearrange("p (g r) -> p r g", g=2), AX.X, ALU.add
                          ).then_inc(self.gathered, 1)
        dve.wait_ge(self.constants_ready, 3)
        self.walk(dve, slot, fills)

    def run(self):
        with self.nc.Block() as block:
            @block.sync
            def _(sync):
                self.sync(sync)

            @block.gpsimd
            def _(pool):
                self.pool(pool)

            @block.tensor
            def _(pe):
                self.tensor(pe)

            @block.scalar
            def _(act):
                self.scalar(act)

            @block.vector
            def _(dve):
                self.vector(dve)


def cross_attention(nc, dram, psum, ident, x):
    with ExitStack() as ctx:
        names = Names(nc, ctx, "cross")
        zt = names.sb("zt", [P, DC, TOKENS])
        ct = names.sb("ct", [CK, 2, BATCH * KEYS])
        gx, bx = names.sb("gx", [P, DC]), names.sb("bx", [P, DC])
        gc, bc = names.sb("gc", [CK, 2]), names.sb("bc", [CK, 2])
        affine_in, ctx_in, wo_in = names.sem("affine_in"), names.sem("ctx_in"), names.sem("wo_in")
        v = names.sb("v", [P, CTX_TILES, HEADS * WIDE])
        with ExitStack() as early:
            inner = Names(nc, early, "cross_early")
            wv = inner.sb("wv", [CK, 2, HEADS * WIDE])
            wv_parts = [inner.sb(f"wv_{part}", [CK, 2, HEADS * WIDE], F32R) for part in ("high", "low")]
            wv_in = inner.sem("wv_in")
            y = inner.sb("y", [P, TILES, DIM])
            ctx_rows = inner.sb("ctx", [P, CTX_TILES, CTX])
            c = [inner.sb(f"c_{part}", [CK, 2, BATCH * KEYS], F32R) for part in ("high", "low")]
            high_ready = inner.sem("high_ready")

            def loads(sync):
                sync.dma_start(ctx_rows[:], dram["ctx"].rearrange("(t p) d -> p t d", p=P)).then_inc(ctx_in, 16)
                for dst, name in ((gx, "g_x"), (bx, "b_x"), (gc, "g_c"), (bc, "b_c")):
                    sync.dma_start(dst[:], dram[f"L0_xattn_{name}"]).then_inc(affine_in, 16)
                sync.dma_start(wv[:], dram["L0_xattn_Wv"]).then_inc(wv_in, 16)

            norm(nc, "cross_norm_c", psum, ident, ctx_rows, CTX, 1e-5, out_feat=ct, kw=CK, gain=gc, shift=bc,
                 loads=loads, loaded=(affine_in, 64), src_in=(ctx_in, 16))
            halves = [(parts, src, k) for parts, src in ((wv_parts, wv), (c, ct)) for k in range(2)]
            with nc.Block() as block:
                @block.scalar
                def _(act):
                    act.wait_ge(wv_in, 16)
                    for parts, src, k in halves:
                        act.activation(parts[0][:, k, :], src[:, k, :], ACT.Copy).then_inc(high_ready, 1)

                @block.vector
                def _(dve):
                    for n, (parts, src, k) in enumerate(halves):
                        dve.wait_ge(high_ready, n + 1)
                        dve.tensor_tensor(parts[1][:, k, :], src[:, k, :], parts[0][:, k, :].bitcast(F32), ALU.subtract)

            values = Values(nc, inner, psum, c, v, wv_parts)
            norm(nc, "cross_norm", psum, ident, x, DIM, 1e-5, out_tok=y, beside=values.programs(0, 8))
            norm(nc, "cross_norm_x", psum, ident, y, DIM, 1e-5, out_feat=zt, gain=gx, shift=bx,
                 loaded=(affine_in, 64), beside=values.programs(8, 18))
            tensor, scalar = values.programs(18, len(values.fills))
            with nc.Block() as block:
                @block.tensor
                def _(pe):
                    tensor(pe)

                @block.scalar
                def _(act):
                    scalar(act)
        with ExitStack() as streaming:
            WideAttention(nc, Names(nc, streaming, "wide"), psum, ident, zt, ct, v, dram).run()
        wo = names.sb("wo", [P, HEADS * WIDE // P, DIM])
        attended = [v[:, t // SEQ_TILES * (KEYS // P) + t % SEQ_TILES, :] for t in range(TILES)]
        project(nc, names, psum, ident, attended, wo, (wo_in, 16), x, load=dram["L0_xattn_Wo"])


class Values:

    def __init__(self, nc, names, psum, c, v, parts):
        self.bank, self.c, self.v, self.parts = psum.banks[4:], c, v, parts
        self.made, self.taken = names.sem("values_made"), names.sem("values_taken")
        self.fills = [(t, half) for t in range(CTX_TILES) for half in range(HEADS * WIDE // BANK)]

    def programs(self, first, stop):
        def tensor(pe):
            for n, (t, half) in list(enumerate(self.fills))[first:stop]:
                if n >= 4:
                    pe.wait_ge(self.taken, n - 3)
                terms = [(k, i, j) for k in range(2) for i, j in ((0, 0), (0, 1), (1, 0))]
                for m, (k, i, j) in enumerate(terms):
                    last = pe.matmul(self.bank[n % 4], self.c[i][:, k, t * P:(t + 1) * P],
                                     self.parts[j][:, k, half * BANK:(half + 1) * BANK],
                                     start=m == 0, stop=m == len(terms) - 1)
                last.then_inc(self.made, 1)

        def scalar(act):
            for n, (t, half) in list(enumerate(self.fills))[first:stop]:
                act.wait_ge(self.made, n + 1)
                act.activation(self.v[:, t, half * BANK:(half + 1) * BANK], self.bank[n % 4], ACT.Copy
                               ).then_inc(self.taken, 1)

        return tensor, scalar


def product_key_experts(nc, dram, psum, ident, x):
    bank = psum.banks
    sides = 2 * PK_HEADS
    slots = EXPERTS // P
    cols = 16
    blocks = P // 2 // cols
    with ExitStack() as ctx:
        names = Names(nc, ctx, "picks")
        yt = names.sb("yt", [P, DC, TOKENS])
        down = names.sb("down", [P, DC, EXPERTS])
        up = names.sb("up", [P, slots, DIM])
        chosen = names.sb("chosen", [P, TILES + 1, 3, P // 2])
        gates = names.sb("gates", [P, slots, SEQ])
        made, gelued = names.sem("made"), names.sem("gelued")
        iota_side = names.sb("iota_side", [P, PK_KEYS])
        wq_in, keys_in, bn_in = names.sem("wq_in"), names.sem("keys_in"), names.sem("bn_in")
        down_in, up_in = names.sem("down_in"), names.sem("up_in")

        with ExitStack() as early:
            inner = Names(nc, early, "picks_early")
            xnt = inner.sb("xnt", [P, DC, TOKENS])
            fused = inner.sb("fused", [P, DC, sides * PK_KEYS])
            with ExitStack() as earliest:
                first = Names(nc, earliest, "picks_first")
                wq = first.sb("wq", [P, sides, DIM])
                keys = first.sb("keys", [P, sides, PK_KEYS])
                gamma, beta = first.sb("gamma", [P, DC]), first.sb("beta", [P, DC])

                def loads(sync):
                    sync.dma_start(wq[:], dram["L0_ffn_w_q"]).then_inc(wq_in, 16)
                    sync.dma_start(keys[:], dram["L0_ffn_keys_p"]).then_inc(keys_in, 16)
                    sync.dma_start(gamma[:], dram["L0_ffn_bn_gamma"]).then_inc(bn_in, 16)
                    sync.dma_start(beta[:], dram["L0_ffn_bn_beta"]).then_inc(bn_in, 16)
                    sync.dma_start(down[:], dram["L0_ffn_down"]).then_inc(down_in, 16)
                    sync.dma_start(up[:], dram["L0_ffn_up"]).then_inc(up_in, 16)

                norm(nc, "picks_norm", psum, ident, x, DIM, 1e-5, out_feat=yt, loads=loads)
                batch_norm_and_keys(nc, first, bank, yt, xnt, fused, wq, keys, gamma, beta,
                                    wq_in, keys_in, bn_in, iota_side)
            pick(nc, inner, psum, ident, xnt, fused, chosen, iota_side, yt, down, gates, down_in, made, gelued)

        deep = 4
        row_numbers = names.sb("row_numbers", [P, P])
        col_numbers = names.sb("col_numbers", [P, 2 * slots])
        high = names.sb("high", [P, TILES, P // 2])
        rows_hot = names.sb("rows_hot", [P, deep, cols, P])
        cols_hot = names.sb("cols_hot", [P, deep, cols, 2 * slots])
        numbered, placed = names.sem("numbered"), names.sem("placed")
        rows_compared, cols_ready = names.sem("rows_compared"), names.sem("cols_ready")
        rows_ready = names.sem("rows_ready")
        weights_made, weighed = names.sem("weights_made"), names.sem("weighed")
        summed, added = names.sem("summed"), names.sem("added")
        n_blocks = SEQ_TILES * blocks
        assert blocks == deep
        with nc.Block() as block:
            @block.tensor
            def _(pe):
                def weights(tile):
                    for u in range(blocks):
                        block_no = tile * blocks + u
                        pe.wait_ge(cols_ready, block_no + 1)
                        pe.wait_ge(rows_ready, block_no + 1)
                        pe.wait_ge(weighed, block_no + 1)
                        for k in range(cols):
                            at = (k % 8) * 2 * slots
                            last = pe.matmul(bank[4 + 2 * (u % 2) + k // 8][:, at:at + 2 * slots],
                                             rows_hot[:, u, k, :], cols_hot[:, u, k, :], start=True, stop=True)
                        last.then_inc(weights_made, 1)

                def times_up(tile):
                    pe.wait_ge(weighed, (tile + 1) * blocks + 2)
                    if tile >= SEQ_TILES:
                        pe.wait_ge(added, tile - SEQ_TILES + 1)
                    for m in range(slots):
                        at = (tile % SEQ_TILES) * P
                        last = pe.matmul(bank[tile % SEQ_TILES][:, 0:DIM], gates[:, m, at:at + P], up[:, m, :],
                                         start=m == 0, stop=m == slots - 1)
                    last.then_inc(summed, 1)

                pe.wait_ge(up_in, 16)
                for tile in range(TILES):
                    weights(tile)
                    if tile % SEQ_TILES:
                        times_up(tile - 1)
                    if tile % SEQ_TILES == SEQ_TILES - 1:
                        times_up(tile)
                    if tile == SEQ_TILES - 1:
                        for m in range(slots):
                            if m >= 4:
                                pe.wait_ge(gelued, slots + m - 3)
                            for c in range(DC):
                                last = pe.matmul(bank[4 + m % 4], down[:, c, m * P:(m + 1) * P],
                                                 yt[:, c, BANK:2 * BANK], start=c == 0, stop=c == DC - 1)
                            last.then_inc(made, 1)
                        pe.wait_ge(gelued, 2 * slots)

            @block.scalar
            def _(act):
                act.wait_ge(summed, SEQ_TILES)
                for m in range(slots):
                    act.wait_ge(made, slots + m + 1)
                    act.activation(gates[:, m, :], bank[4 + m % 4], ACT.Gelu).then_inc(gelued, 1)

            @block.gpsimd
            def _(pool):
                pool.iota(row_numbers[:], pattern=[[1, P]], base=0, channel_multiplier=0,
                          allow_small_or_imprecise_dtypes=True).then_inc(numbered, 1)
                for side in range(2):
                    pool.wait_ge(numbered, side + 1)
                    pool.iota(col_numbers[side * P // 2:(side + 1) * P // 2, :], pattern=[[1, 2 * slots]],
                              base=-side * slots, channel_multiplier=0,
                              allow_small_or_imprecise_dtypes=True).then_inc(numbered, 1)
                with pool.Fori(0, TILES) as tile:
                    for u in range(deep):
                        pool.wait_ge(rows_compared, tile * deep + u + 1)
                        weight = chosen[:, tile, 2, u * cols:(u + 1) * cols].unsqueeze(2).to_broadcast([P, cols, P])
                        pool.tensor_tensor(rows_hot[:, u], rows_hot[:, u], weight, ALU.mult).then_inc(rows_ready, 1)

            @block.vector
            def _(dve):
                primer = names.sb("primer", [P, 3])
                for n in range(2):
                    dve.memset(primer[:, n:n + 1], 0.0).then_inc(weighed, 1)
                chain = Chain(dve, placed)
                dve.memset(chosen[:, TILES], 0.0)
                first, second = chosen[:, 0:TILES, 0, :], chosen[:, 0:TILES, 1, :]
                chain.link(dve.tensor_scalar(high[:], second, float(slots), float(PK_KEYS), ALU.is_ge, ALU.mult))
                dve.tensor_tensor(first, first, high[:], ALU.add)
                chain.link(dve.scalar_tensor_tensor(out=second, in0=high[:], scalar=-slots / PK_KEYS, in1=second,
                                                    op0=ALU.mult, op1=ALU.add))
                dve.wait_ge(numbered, 3)

                def hot(tile, u):
                    for buffer, row, numbers, done in ((rows_hot, 0, row_numbers, rows_compared),
                                                       (cols_hot, 1, col_numbers, cols_ready)):
                        shape = [P, cols, numbers.shape[1]]
                        picks = chosen[:, tile, row, u * cols:(u + 1) * cols].unsqueeze(2).to_broadcast(shape)
                        dve.tensor_tensor(buffer[:, u], picks, numbers[:].unsqueeze(1).to_broadcast(shape),
                                          ALU.is_equal).then_inc(done, 1)

                hot(0, 0)
                hot(0, 1)
                with dve.Fori(0, BATCH) as b:
                    hold(dve, gelued, b * slots + slots, primer[:, 2:3])
                    with dve.Fori(0, SEQ_TILES) as turn:
                        tile = b * SEQ_TILES + turn
                        for u in range(deep):
                            hot(tile + (u + 2) // deep, (u + 2) % deep)
                            dve.wait_ge(weights_made, tile * blocks + u + 1)
                            tokens = gates[:, :, bass.ds(turn * P, P)].rearrange(
                                "p m (s k) -> p k s m", s=2)[:, u * cols:(u + 1) * cols]
                            pair = psum.all[:, (4 + 2 * (u % 2)) * BANK:(6 + 2 * (u % 2)) * BANK]
                            dve.tensor_tensor(tokens, tokens, pair.rearrange("p (k s m) -> p k s m", s=2, m=slots),
                                              ALU.mult).then_inc(weighed, 1)
                    for tile in range(SEQ_TILES):
                        dve.wait_ge(summed, b * SEQ_TILES + tile + 1)
                        rows = x[:, bass.ds(b * SEQ_TILES + tile, 1), :].rearrange("p t d -> p (t d)")
                        dve.tensor_tensor(rows, rows, bank[tile][:, 0:DIM], ALU.add).then_inc(added, 1)


def batch_norm_and_keys(nc, names, bank, yt, xnt, fused, wq, keys, gamma, beta, wq_in, keys_in, bn_in, iota_side):
    sides = 2 * PK_HEADS
    stats = names.sb("bn_stats", [P, DC, TOKENS // BANK, 6])
    moments = names.sb("bn_moments", [P, DC, 2])
    spread = names.sb("bn_spread", [P, DC])
    root = names.sb("bn_root", [P, DC])
    gain = names.sb("bn_gain", [P, DC])
    shift = names.sb("bn_shift", [P, DC])
    dve_steps = names.sem("bn_steps")
    spread_ready, root_ready = names.sem("bn_spread_ready"), names.sem("bn_root_ready")
    fused_made = names.sem("fused_made")
    with nc.Block() as block:
        @block.gpsimd
        def _(pool):
            pool.iota(iota_side[:], pattern=[[1, PK_KEYS]], base=0, channel_multiplier=0,
                      allow_small_or_imprecise_dtypes=True)

        @block.tensor
        def _(pe):
            pe.wait_ge(wq_in, 16)
            pe.wait_ge(keys_in, 16)
            for c in range(DC):
                for side in range(sides):
                    n, k = divmod(c * sides + side, 8)
                    last = pe.matmul(bank[n][:, k * PK_KEYS:(k + 1) * PK_KEYS], wq[:, side, c * P:(c + 1) * P],
                                     keys[:, side, :], start=True, stop=True)
                    if k == 7:
                        last.then_inc(fused_made, 1)

        @block.scalar
        def _(act):
            act.wait_ge(spread_ready, 1)
            act.activation(root[:], spread[:], ACT.Sqrt).then_inc(root_ready, 1)
            for n in range(DC * sides // 8):
                c, part = divmod(n, sides // 8)
                act.wait_ge(fused_made, n + 1)
                act.activation(fused[:, c, part * BANK:(part + 1) * BANK], bank[n], ACT.Copy)

        @block.vector
        def _(dve):
            chain = Chain(dve, dve_steps)
            for c in range(DC):
                for n in range(TOKENS // BANK):
                    last = dve.bn_stats(stats[:, c, n, :], yt[:, c, n * BANK:(n + 1) * BANK])
            chain.link(last)
            for c in range(DC):
                last = dve.bn_aggr(moments[:, c, :], stats[:, c].rearrange("p n s -> p (n s)"))
            chain.link(last)
            dve.tensor_scalar(spread[:], moments[:, :, 1], 1e-5, None, ALU.add).then_inc(spread_ready, 1)
            dve.wait_ge(root_ready, 1)
            dve.wait_ge(bn_in, 32)
            chain.link(dve.reciprocal(gain[:], root[:]))
            chain.link(dve.tensor_tensor(gain[:], gain[:], gamma[:], ALU.mult))
            chain.link(dve.tensor_tensor(shift[:], moments[:, :, 0], gain[:], ALU.mult))
            chain.link(dve.tensor_tensor(shift[:], beta[:], shift[:], ALU.subtract))
            for c in range(DC):
                dve.tensor_scalar(xnt[:, c, :], yt[:, c, :], gain[:, c:c + 1], shift[:, c:c + 1], ALU.mult, ALU.add)


def pick(nc, names, psum, ident, xnt, fused, chosen, iota_side, yt, down, gates, down_in, made, gelued):
    bank = psum.banks
    pairs = [psum.all[:, 2 * n * BANK:2 * (n + 1) * BANK] for n in range(2)]
    sides, H = 2 * PK_HEADS, PK_HEADS
    scores = names.sb("scores", [P, 2, sides, PK_KEYS])
    best = names.sb("best", [P, 2, sides, TOP])
    which = names.sb("which", [P, 2, sides, TOP], U32)
    which_f = names.sb("which_f", [P, 2, sides, TOP])
    pair_sums = names.sb("pair_sums", [P, 2, H, TOP * TOP])
    pair_best = names.sb("pair_best", [P, 2, H, TOP])
    pair_at = names.sb("pair_at", [P, 2, H * TOP], U32)
    pair_side = names.sb("pair_side", [P, 2, 2, H * TOP], U32)
    pair_side_f = names.sb("pair_side_f", [P, 2, 2, H * TOP])
    hit = names.sb("hit", [P, 2, 2, H, TOP, TOP])
    found = names.sb("found", [P, 2, 3, 2, PICKS])
    scores_made, scores_ready, best_ready = names.sem("scores_made"), names.sem("scores_ready"), names.sem("best_ready")
    found_ready, turned, taken = names.sem("found_ready"), names.sem("turned"), names.sem("taken")
    dve_steps = names.sem("pick_steps")
    scratch = names.sb("scratch", [P, 3])
    turns = TILES // 2
    some = EXPERTS // P // turns
    with nc.Block() as block:
        @block.scalar
        def _(act):
            def take_scores(tile):
                u = tile % 2
                act.wait_ge(scores_made, tile + 1)
                if tile >= 2:
                    act.wait_ge(best_ready, tile - 1)
                act.activation(scores[:, u].rearrange("p s k -> p (s k)"), pairs[u], ACT.Copy
                               ).then_inc(scores_ready, 1)

            take_scores(0)
            take_scores(1)
            for pair in range(turns):
                tiles = (2 * pair, 2 * pair + 1)
                for m in range(pair * some, pair * some + some):
                    if m % some == some // 2 and pair + 1 < turns:
                        for tile in tiles:
                            take_scores(tile + 2)
                    act.wait_ge(made, m + 1)
                    act.activation(gates[:, m, :], bank[6 + m % 2], ACT.Gelu).then_inc(gelued, 1)
                for tile in tiles:
                    act.wait_ge(turned, tile + 3)
                    for half in range(2):
                        r = slice(64 * half, 64 * half + 64)
                        last = act.activation(
                            chosen[r, tile, :, :],
                            bank[4 + tile % 2][r, 0:3 * P].rearrange("p (k c) -> p k c", c=P)[:, :, 64 * half:64 * half + 64],
                            ACT.Copy)
                    last.then_inc(taken, 1)
            act.wait_ge(taken, TILES)
            act.activation(chosen[:, 0:TILES, 2, :], chosen[:, 0:TILES, 2, :], ACT.Sigmoid)

        @block.tensor
        def _(pe):
            def score(tile):
                u = tile % 2
                if tile >= 2:
                    pe.wait_ge(scores_ready, tile - 1)
                for part in range(2):
                    for c in range(DC):
                        last = pe.matmul(bank[2 * u + part], xnt[:, c, tile * P:(tile + 1) * P],
                                         fused[:, c, part * BANK:(part + 1) * BANK], start=c == 0, stop=c == DC - 1)
                last.then_inc(scores_made, 1)

            score(0)
            score(1)
            pe.wait_ge(down_in, 16)
            for pair in range(turns):
                tiles = (2 * pair, 2 * pair + 1)
                if pair + 1 < turns:
                    for tile in tiles:
                        score(tile + 2)
                for m in range(pair * some, pair * some + some):
                    if m >= 2:
                        pe.wait_ge(gelued, m - 1)
                    for c in range(DC):
                        last = pe.matmul(bank[6 + m % 2], down[:, c, m * P:(m + 1) * P], yt[:, c, 0:BANK],
                                         start=c == 0, stop=c == DC - 1)
                    last.then_inc(made, 1)
                for tile in tiles:
                    pe.wait_ge(found_ready, tile + 1)
                    if tile >= 2:
                        pe.wait_ge(taken, tile - 1)
                    for k in range(3):
                        last = pe.transpose(bank[4 + tile % 2][:, k * P:(k + 1) * P],
                                            found[:, tile % 2, k].rearrange("p a b -> p (a b)"), ident[:])
                    last.then_inc(turned, 1)

        @block.vector
        def _(dve):
            for n in range(2):
                dve.memset(scratch[:, n + 1:n + 2], 0.0).then_inc(turned, 1)
            four = [P, H, TOP, TOP]
            places = iota_side[:, 0:TOP].unsqueeze(1).to_broadcast([P, PICKS, TOP])
            with dve.Fori(0, turns) as turn:
                chain = Chain(dve, dve_steps, turn, 10)
                hold(dve, scores_ready, turn * 2 + 2, scratch[:, 0:1])
                for u in range(2):
                    for s in range(sides):
                        last = dve.max(best[:, u, s, :], scores[:, u, s, :])
                chain.link(last, scratch[:, 0:1])
                for u in range(2):
                    for s in range(sides):
                        last = dve.max_index(which[:, u, s, :], best[:, u, s, :], scores[:, u, s, :])
                chain.link(last)
                for u in range(2):
                    dve.tensor_copy(which_f[:, u], which[:, u]).then_inc(best_ready, 1)
                for u in range(2):
                    last = dve.tensor_tensor(pair_sums[:, u].rearrange("p h (a b) -> p h a b", b=TOP),
                                             best[:, u, 0:H, :].unsqueeze(3).to_broadcast(four),
                                             best[:, u, H:, :].unsqueeze(2).to_broadcast(four), ALU.add)
                chain.link(last, scratch[:, 0:1])
                for u in range(2):
                    for h in range(H):
                        last = dve.max(pair_best[:, u, h, :], pair_sums[:, u, h, :])
                chain.link(last, scratch[:, 0:1])
                for u in range(2):
                    for h in range(H):
                        last = dve.max_index(pair_at[:, u, h * TOP:(h + 1) * TOP], pair_best[:, u, h, :],
                                             pair_sums[:, u, h, :])
                chain.link(last)
                for u in range(2):
                    dve.tensor_scalar(pair_side[:, u, 0, :], pair_at[:, u, :], 3, None, ALU.logical_shift_right)
                    last = dve.tensor_scalar(pair_side[:, u, 1, :], pair_at[:, u, :], 7, None, ALU.bitwise_and)
                chain.link(last)
                chain.link(dve.tensor_copy(pair_side_f[:], pair_side[:]))
                for u in range(2):
                    for side in range(2):
                        last = dve.tensor_tensor(hit[:, u, side].rearrange("p h k n -> p (h k) n"),
                                                 pair_side_f[:, u, side, :].unsqueeze(2).to_broadcast([P, PICKS, TOP]),
                                                 places, ALU.is_equal)
                chain.link(last)
                for u in range(2):
                    for side in range(2):
                        keys_of = which_f[:, u, side * H:(side + 1) * H, :].unsqueeze(2).to_broadcast(four)
                        last = dve.tensor_tensor(hit[:, u, side], hit[:, u, side], keys_of, ALU.mult)
                chain.link(last)
                for u in range(2):
                    dve.wait_ge(turned, turn * 2 + u + 1)
                    dve.tensor_copy(found[:, u, 2].rearrange("p c (h k) -> p c h k", k=TOP),
                                    pair_best[:, u].unsqueeze(1).to_broadcast([P, 2, H, TOP]))
                    for side in range(2):
                        last = dve.tensor_reduce(found[:, u, side, 0, :], hit[:, u, side].rearrange("p h k n -> p (h k) n"),
                                                 AX.X, ALU.add)
                chain.link(last)
                for u in range(2):
                    dve.tensor_copy(found[:, u, 0:2, 1, :], found[:, u, 0:2, 0, :]).then_inc(found_ready, 1)
                chain.end()


def gated_scan(nc, dram, psum, ident, x):
    bank = psum.banks
    with ExitStack() as ctx:
        names = Names(nc, ctx, "scan")
        y = names.sb("y", [P, TILES, DIM])
        xnt = names.sb("xnt", [P, DC, TOKENS])
        gains = names.sb("gains", [P, 2, DC])
        w_fc = names.sb("w_fc", [P, DC, FF])
        w_fcact = names.sb("w_fcact", [P, DC, FF])
        w_out = names.sb("w_out", [P, FF // P, DIM])
        b_ff = names.sb("b_ff", [P, 2, FF // P])
        b_out = names.sb("b_out", [P, DIM])
        gains_in, square_in, ff_in = names.sem("gains_in"), names.sem("square_in"), names.sem("ff_in")

        with ExitStack() as early:
            inner = Names(nc, early, "scan_early")
            kinds = ("ln_z", "dt", "yact", "y")
            w = {k: inner.sb(f"w_{k}", [P, DC, DIM]) for k in kinds}
            bias = {k: inner.sb(f"b_{k}", [P, DC]) for k in kinds}
            h0 = inner.sb("h0", [P, DC])
            minus_dt = inner.sb("minus_dt", [P, DC])
            open_z = inner.sb("open_z", [P, DC, TOKENS])
            open_dt = inner.sb("open_dt", [P, DC, TOKENS])
            keep = inner.sb("keep", [P, DC, TOKENS])
            act_y = inner.sb("act_y", [P, DC, TOKENS])
            h = inner.sb("h", [P, DC, TOKENS])
            gated = inner.sb("gated", [P, DC, TOKENS])
            made, acted, negated = inner.sem("made"), inner.sem("acted"), inner.sem("negated")
            scanned, y_made, gated_ready = inner.sem("scanned"), inner.sem("y_made"), inner.sem("gated_ready")
            turned, added, dve_steps = inner.sem("turned"), inner.sem("added"), inner.sem("dve_steps")

            def loads(sync):
                sync.dma_start(gains[:], dram["L1_attn_gains"]).then_inc(gains_in, 16)
                for k in kinds:
                    sync.dma_start(w[k][:], dram[f"L1_attn_w_{k}"]).then_inc(square_in, 16)
                    sync.dma_start(bias[k][:], dram[f"L1_attn_b_{k}"]).then_inc(square_in, 16)
                sync.dma_start(h0[:], dram["L1_attn_h0"]).then_inc(square_in, 16)
                sync.dma_start(w_fc[:], dram["L1_attn_w_fc"]).then_inc(ff_in, 16)
                sync.dma_start(w_fcact[:], dram["L1_attn_w_fcact"]).then_inc(ff_in, 16)
                sync.dma_start(w_out[:], dram["L1_attn_w_out"]).then_inc(ff_in, 16)
                sync.dma_start(b_ff[:], dram["L1_attn_b_ff"]).then_inc(ff_in, 16)
                load_row(sync, b_out[:], dram["L1_attn_b_out"], ff_in)

            norm(nc, "scan_norm", psum, ident, x, DIM, 1e-5, out_tok=y, loads=loads)
            norm(nc, "scan_rms", psum, ident, y, DIM, 1e-6, centre=False, out_feat=xnt, gain=gains[:, 0],
                 loaded=(gains_in, 16))

            spots = [(m, b) for m in range(DC) for b in range(BATCH)]
            with nc.Block() as block:
                @block.tensor
                def _(pe):
                    pe.wait_ge(square_in, 16 * 9)
                    n = 0
                    for k in ("ln_z", "dt", "yact"):
                        for m, b in spots:
                            if n >= 4:
                                pe.wait_ge(acted, n - 3)
                            for c in range(DC):
                                last = pe.matmul(bank[n % 4], w[k][:, c, m * P:(m + 1) * P],
                                                 xnt[:, c, b * BANK:(b + 1) * BANK], start=c == 0, stop=c == DC - 1)
                            last.then_inc(made, 1)
                            n += 1
                    pe.wait_ge(scanned, 4)
                    for n, (m, b) in enumerate(spots):
                        for c in range(DC):
                            last = pe.matmul(bank[4 + n], w["y"][:, c, m * P:(m + 1) * P],
                                             h[:, c, b * BANK:(b + 1) * BANK], start=c == 0, stop=c == DC - 1)
                        last.then_inc(y_made, 1)
                    pe.wait_ge(gated_ready, 4)
                    pe.wait_ge(acted, 12)
                    for pair in range(TILES // 2):
                        for k in range(4):
                            t, c = 2 * pair + k // 2, k % 2
                            last = pe.transpose(bank[pair][:, k * P:(k + 1) * P], gated[:, c, t * P:(t + 1) * P], ident[:])
                        last.then_inc(turned, 1)

                @block.scalar
                def _(act):
                    act.wait_ge(negated, 1)
                    n = 0
                    for m, b in spots:
                        act.wait_ge(made, n + 1)
                        act.activation(open_z[:, m, b * BANK:(b + 1) * BANK], bank[n % 4], ACT.Sigmoid,
                                       bias=bias["ln_z"][:, m:m + 1]).then_inc(acted, 1)
                        n += 1
                    for m, b in spots:
                        act.wait_ge(made, n + 1)
                        act.activation(open_dt[:, m, b * BANK:(b + 1) * BANK], bank[n % 4], ACT.Sigmoid,
                                       bias=bias["dt"][:, m:m + 1])
                        act.activation(keep[:, m, b * BANK:(b + 1) * BANK], bank[n % 4], ACT.Sigmoid,
                                       bias=minus_dt[:, m:m + 1], scale=-1.0).then_inc(acted, 1)
                        n += 1
                    for m, b in spots:
                        act.wait_ge(made, n + 1)
                        act.activation(act_y[:, m, b * BANK:(b + 1) * BANK], bank[n % 4], ACT.Silu,
                                       bias=bias["yact"][:, m:m + 1]).then_inc(acted, 1)
                        n += 1

                @block.vector
                def _(dve):
                    chain = Chain(dve, dve_steps)
                    dve.wait_ge(square_in, 16 * 9)
                    dve.tensor_scalar(minus_dt[:], bias["dt"][:], -1.0, None, ALU.mult).then_inc(negated, 1)
                    for n, (m, b) in enumerate(spots):
                        part = slice(b * BANK, (b + 1) * BANK)
                        dve.wait_ge(acted, 4 + n + 1)
                        chain.link(dve.tensor_tensor(open_z[:, m, part], open_z[:, m, part], open_dt[:, m, part], ALU.mult))
                        dve.tensor_tensor_scan(h[:, m, part], keep[:, m, part], open_z[:, m, part], h0[:, m:m + 1],
                                               ALU.mult, ALU.add).then_inc(scanned, 1)
                    for n, (m, b) in enumerate(spots):
                        part = slice(b * BANK, (b + 1) * BANK)
                        dve.wait_ge(acted, 8 + n + 1)
                        dve.wait_ge(y_made, n + 1)
                        dve.scalar_tensor_tensor(out=gated[:, m, part], in0=bank[4 + n], scalar=bias["y"][:, m:m + 1],
                                                 in1=act_y[:, m, part], op0=ALU.add, op1=ALU.mult).then_inc(gated_ready, 1)
                    for pair in range(TILES // 2):
                        both = slice(2 * pair, 2 * pair + 2)
                        dve.wait_ge(turned, pair + 1)
                        dve.tensor_tensor(y[:, both, :], y[:, both, :], by_tile(bank[pair]), ALU.add).then_inc(added, 1)

        norm(nc, "scan_rms_ff", psum, ident, y, DIM, 1e-6, centre=False, out_feat=xnt, gain=gains[:, 1],
             loaded=(gains_in, 16))
        hidden = names.sb("hidden", [P, FF // P, TOKENS])
        act_h = names.sb("act_h", [P, 2, BANK])
        made_act, acted = names.sem("ff_made_act"), names.sem("ff_acted")
        made, multiplied, out_made, stored = (names.sem(n) for n in ("ff_made", "ff_multiplied", "ff_out_made", "ff_stored"))
        steps = names.sem("ff_steps")
        jobs = [(b, f) for b in range(BATCH) for f in range(FF // P)]
        with nc.Block() as block:
            @block.tensor
            def _(pe):
                pe.wait_ge(ff_in, 16 * 5)
                for n, (b, f) in enumerate(jobs):
                    part = slice(b * BANK, (b + 1) * BANK)
                    if n >= 2:
                        pe.wait_ge(acted, n - 1)
                    for c in range(DC):
                        last = pe.matmul(bank[n % 2], w_fcact[:, c, f * P:(f + 1) * P], xnt[:, c, part],
                                         start=c == 0, stop=c == DC - 1)
                    last.then_inc(made_act, 1)
                    if n >= 2:
                        pe.wait_ge(multiplied, n - 1)
                    for c in range(DC):
                        last = pe.matmul(bank[2 + n % 2], w_fc[:, c, f * P:(f + 1) * P], xnt[:, c, part],
                                         start=c == 0, stop=c == DC - 1)
                    last.then_inc(made, 1)
                pe.wait_ge(multiplied, len(jobs))
                for t in range(TILES):
                    for f in range(FF // P):
                        last = pe.matmul(bank[4 + t // 2][:, (t % 2) * DIM:(t % 2 + 1) * DIM],
                                         hidden[:, f, t * P:(t + 1) * P], w_out[:, f, :], start=f == 0,
                                         stop=f == FF // P - 1)
                    if t % 2:
                        last.then_inc(out_made, 1)

            @block.scalar
            def _(act):
                act.wait_ge(ff_in, 16 * 5)
                for n, (b, f) in enumerate(jobs):
                    act.wait_ge(made_act, n + 1)
                    if n >= 2:
                        act.wait_ge(multiplied, n - 1)
                    act.activation(act_h[:, n % 2, :], bank[n % 2], ACT.Silu, bias=b_ff[:, 1, f:f + 1]).then_inc(acted, 1)

            @block.vector
            def _(dve):
                chain = Chain(dve, steps)
                dve.wait_ge(ff_in, 16 * 5)
                chain.link(dve.tensor_tensor(x[:], x[:], y[:], ALU.add))
                chain.link(dve.tensor_tensor(x[:], x[:], over_tiles(b_out, TILES), ALU.add))
                for n, (b, f) in enumerate(jobs):
                    dve.wait_ge(acted, n + 1)
                    dve.wait_ge(made, n + 1)
                    dve.scalar_tensor_tensor(out=hidden[:, f, b * BANK:(b + 1) * BANK], in0=bank[2 + n % 2],
                                             scalar=b_ff[:, 0, f:f + 1], in1=act_h[:, n % 2, :], op0=ALU.add,
                                             op1=ALU.mult).then_inc(multiplied, 1)
                for pair in range(TILES // 2):
                    both = slice(2 * pair, 2 * pair + 2)
                    dve.wait_ge(out_made, pair + 1)
                    dve.tensor_tensor(x[:, both, :], x[:, both, :], by_tile(bank[4 + pair]), ALU.add).then_inc(stored, 1)


def small_cross_attention(nc, dram, psum, ident, x):
    bank = psum.banks
    with ExitStack() as ctx:
        names = Names(nc, ctx, "small")
        qh, ql = names.sb("qh", [P, TILES, DIM], F32R), names.sb("ql", [P, TILES, DIM], F32R)
        kh, kl = names.sb("kh", [P, CTX_TILES, DIM], F32R), names.sb("kl", [P, CTX_TILES, DIM], F32R)
        wo = names.sb("wo", [P, DC, DIM])
        wo_in = names.sem("wo_in")
        kv = names.sb("kv", [P, CTX_TILES, 2 * DIM])
        with ExitStack() as early:
            inner = Names(nc, early, "small_early")
            yt = inner.sb("yt", [P, DC, TOKENS])
            ct = inner.sb("ct", [CK, 2, BATCH * KEYS])
            wq = inner.sb("wq", [P, DC, DIM])
            wkv = inner.sb("wkv", [CK, 2, 2 * DIM])
            bq, bkv, bo = inner.sb("bq", [P, DIM]), inner.sb("bkv", [P, 2 * DIM]), inner.sb("bo", [P, DIM])
            loaded = inner.sem("loaded")
            q = inner.sb("q", [P, TILES, DIM])
            k_high, q_high = inner.sem("k_high"), inner.sem("q_high")
            kv_made, kv_ready, q_made, q_ready = (inner.sem(n) for n in ("kv_made", "kv_ready", "q_made", "q_ready"))

            def loads(sync):
                for dst, name in ((ct, "ctx_t"), (wkv, "L1_xattn_kv_w"), (wq, "L1_xattn_q_w")):
                    sync.dma_start(dst[:], dram[name]).then_inc(loaded, 16)
                sync.dma_start(wo[:], dram["L1_xattn_proj_w"]).then_inc(wo_in, 16)
                for dst, name in ((bkv, "kv_b"), (bq, "q_b"), (bo, "proj_b")):
                    load_row(sync, dst[:], dram[f"L1_xattn_{name}"], loaded)

            norm(nc, "small_norm", psum, ident, x, DIM, 1e-5, out_feat=yt, loads=loads)
            with nc.Block() as block:
                @block.tensor
                def _(pe):
                    pe.wait_ge(loaded, 16 * 6)
                    for t in range(CTX_TILES):
                        if t >= 4:
                            pe.wait_ge(kv_ready, t - 3)
                        for c in range(2):
                            last = pe.matmul(bank[t % 4], ct[:, c, t * P:(t + 1) * P], wkv[:, c, :], start=c == 0,
                                             stop=c == 1)
                        last.then_inc(kv_made, 1)
                    for t in range(TILES):
                        for c in range(DC):
                            last = pe.matmul(bank[4 + t // 2][:, (t % 2) * DIM:(t % 2 + 1) * DIM],
                                             yt[:, c, t * P:(t + 1) * P], wq[:, c, :], start=c == 0, stop=c == DC - 1)
                        if t % 2:
                            last.then_inc(q_made, 1)

                @block.vector
                def _(dve):
                    dve.wait_ge(loaded, 16 * 6)
                    for t in range(CTX_TILES):
                        dve.wait_ge(kv_made, t + 1)
                        dve.tensor_tensor(kv[:, t, :], bank[t % 4], bkv[:], ALU.add).then_inc(kv_ready, 1)
                    for pair in range(TILES // 2):
                        dve.wait_ge(q_made, pair + 1)
                        dve.tensor_tensor(q[:, 2 * pair:2 * pair + 2, :], by_tile(bank[4 + pair]), over_tiles(bq, 2),
                                          ALU.add).then_inc(q_ready, 1)
                    for pair in range(TILES // 2):
                        some = slice(2 * pair, 2 * pair + 2)
                        dve.wait_ge(q_high, pair + 1)
                        dve.scalar_tensor_tensor(out=ql[:, some, :], in0=q[:, some, :], scalar=HEAD ** -0.5,
                                                 in1=qh[:, some, :].bitcast(F32), op0=ALU.mult, op1=ALU.subtract)
                    dve.tensor_tensor(x[:], x[:], over_tiles(bo, TILES), ALU.add)

                @block.scalar
                def _(act):
                    for t in range(CTX_TILES):
                        act.wait_ge(kv_ready, t + 1)
                        act.activation(kh[:, t, :], kv[:, t, 0:DIM], ACT.Copy).then_inc(k_high, 1)
                    for pair in range(TILES // 2):
                        some = slice(2 * pair, 2 * pair + 2)
                        act.wait_ge(q_ready, pair + 1)
                        act.activation(qh[:, some, :], q[:, some, :], ACT.Copy, scale=HEAD ** -0.5).then_inc(q_high, 1)

                @block.gpsimd
                def _(pool):
                    for t in range(CTX_TILES):
                        pool.wait_ge(k_high, t + 1)
                        pool.tensor_tensor(kl[:, t, :], kv[:, t, 0:DIM], kh[:, t, :].bitcast(F32), ALU.subtract)

        attended = names.sb("attended", [P, TILES, DIM])
        StreamedAttention(nc, names, psum, ident, qh, ql, kh, kl, kv[:, :, DIM:], attended, KEYS).run()
        project(nc, names, psum, ident, [attended[:, t, :] for t in range(TILES)], wo,
                (wo_in, 16), x)


def last_block(nc, dram, psum, ident, x):
    with ExitStack() as ctx:
        names = Names(nc, ctx, "last")
        y = names.sb("y", [P, TILES, DIM])
        gains = names.sb("gains", [P, 2, DC])
        gains_in = names.sem("gains_in")
        with ExitStack() as early:
            inner = Names(nc, early, "heads")
            qkv = inner.sb("qkv", [P, TILES, 3 * DIM])
            high = inner.sb("high", [P, TILES, 2 * DIM], F32R)
            low = inner.sb("low", [P, TILES, 2 * DIM], F32R)
            wo = inner.sb("wo", [P, DC, DIM])
            wo_in = inner.sem("wo_in")
            attended = inner.sb("attended", [P, TILES, DIM])
            normed_heads(nc, dram, psum, ident, x, y, qkv, high, low, gains, gains_in, wo, wo_in)
            StreamedAttention(nc, inner, psum, ident, high[:, :, 0:DIM], low[:, :, 0:DIM], high[:, :, DIM:],
                              low[:, :, DIM:], qkv[:, :, 2 * DIM:], attended, SEQ, causal=True).run()
            project(nc, inner, psum, ident, [attended[:, t, :] for t in range(TILES)], wo,
                    (wo_in, 16), y, add_from=MASKED)
        mixture(nc, dram, psum, ident, x, y, gains, gains_in)


def normed_heads(nc, dram, psum, ident, x, y, qkv, high, low, gains, gains_in, wo, wo_in):
    bank = psum.banks
    with ExitStack() as ctx:
        names = Names(nc, ctx, "heads_early")
        ht = names.sb("ht", [P, DC, TOKENS])
        w = names.sb("w", [P, DC, 3 * DIM])
        head_gain = names.sb("head_gain", [P, 2 * HEAD])
        squares = names.sb("squares", [P, TILES, 2 * DIM])
        power = names.sb("power", [P, TILES, 2 * HEADS])
        root = names.sb("root", [P, TILES, 2 * HEADS])
        inverse = names.sb("inverse", [P, TILES, 2 * HEADS])
        loaded = names.sem("loaded")
        made, taken, power_ready, root_ready, steps, rows_ready, high_ready = (
            names.sem(n) for n in ("made", "taken", "power_ready", "root_ready", "steps", "rows_ready", "high_ready"))

        def loads(sync):
            sync.dma_start(gains[:], dram["L1_ffn_gains"]).then_inc(gains_in, 16)
            sync.dma_start(w[:], dram["L1_ffn_wqkv"]).then_inc(loaded, 16)
            load_row(sync, head_gain[:], dram["L1_ffn_head_gain"], loaded)
            sync.dma_start(wo[:], dram["L1_ffn_wo"]).then_inc(wo_in, 16)

        norm(nc, "last_norm", psum, ident, x, DIM, 1e-5, out_tok=y, loads=loads)
        norm(nc, "last_rms", psum, ident, y, DIM, 1.1920929e-07, centre=False, out_feat=ht, gain=gains[:, 0],
             loaded=(gains_in, 16))
        with nc.Block() as block:
            @block.tensor
            def _(pe):
                pe.wait_ge(loaded, 32)
                for t in range(TILES):
                    qk, v = bank[2 * (t % 4)], bank[2 * (t % 4) + 1]
                    if t >= 4:
                        pe.wait_ge(taken, t - 3)
                    for dst, cols in ((qk, slice(0, 2 * DIM)), (v[:, 0:DIM], slice(2 * DIM, 3 * DIM))):
                        for c in range(DC):
                            last = pe.matmul(dst, ht[:, c, t * P:(t + 1) * P], w[:, c, cols], start=c == 0,
                                             stop=c == DC - 1)
                    last.then_inc(made, 1)

            @block.scalar
            def _(act):
                for t in range(TILES):
                    act.wait_ge(made, t + 1)
                    act.activation(qkv[:, t, :], psum.all[:, 2 * (t % 4) * BANK:2 * (t % 4) * BANK + 3 * DIM],
                                   ACT.Copy).then_inc(taken, 1)
                act.wait_ge(power_ready, 1)
                act.activation(root[:], power[:], ACT.Sqrt).then_inc(root_ready, 1)
                for t in range(TILES):
                    act.wait_ge(rows_ready, t + 1)
                    act.activation(high[:, t, 0:DIM], qkv[:, t, 0:DIM], ACT.Copy, scale=HEAD ** -0.5)
                    act.activation(high[:, t, DIM:], qkv[:, t, DIM:2 * DIM], ACT.Copy).then_inc(high_ready, 1)

            @block.gpsimd
            def _(pool):
                for t in range(TILES):
                    pool.wait_ge(high_ready, t + 1)
                    pool.tensor_tensor(low[:, t, DIM:], qkv[:, t, DIM:2 * DIM], high[:, t, DIM:].bitcast(F32), ALU.subtract)

            @block.vector
            def _(dve):
                chain = Chain(dve, steps)
                for t in range(TILES):
                    dve.wait_ge(taken, t + 1)
                    chain.link(dve.tensor_tensor(squares[:, t, :], qkv[:, t, 0:2 * DIM], qkv[:, t, 0:2 * DIM], ALU.mult))
                    last = dve.tensor_reduce(power[:, t, :], squares[:, t, :].rearrange("p (h r) -> p h r", r=HEAD),
                                             AX.X, ALU.add)
                chain.link(last)
                dve.tensor_scalar(power[:], power[:], 1.0 / HEAD, 1.1920929e-07, ALU.mult, ALU.add).then_inc(power_ready, 1)
                dve.wait_ge(root_ready, 1)
                dve.wait_ge(loaded, 32)
                chain.link(dve.reciprocal(inverse[:], root[:]))
                for t in range(TILES):
                    rows = qkv[:, t, 0:2 * DIM].rearrange("p (h r) -> p h r", r=HEAD)
                    last = dve.tensor_tensor(rows, rows, inverse[:, t, :].unsqueeze(2).to_broadcast([P, 2 * HEADS, HEAD]),
                                             ALU.mult)
                chain.link(last)
                for t in range(TILES):
                    rows = qkv[:, t, 0:2 * DIM].rearrange("p (s h r) -> p s h r", s=2, r=HEAD)
                    gain = head_gain[:].rearrange("p (s r) -> p s r", s=2).unsqueeze(2).to_broadcast([P, 2, HEADS, HEAD])
                    dve.tensor_tensor(rows, rows, gain, ALU.mult).then_inc(rows_ready, 1)
                for t in range(TILES):
                    dve.wait_ge(high_ready, t + 1)
                    dve.scalar_tensor_tensor(out=low[:, t, 0:DIM], in0=qkv[:, t, 0:DIM], scalar=HEAD ** -0.5,
                                             in1=high[:, t, 0:DIM].bitcast(F32), op0=ALU.mult, op1=ALU.subtract)


def mixture(nc, dram, psum, ident, x, y, gains, gains_in):
    bank = psum.banks
    with ExitStack() as ctx:
        names = Names(nc, ctx, "mix")
        xt = names.sb("xt", [P, DC, TOKENS])
        shapes = {"e0_up": (DIM, HID), "e0_down": (HID, DIM), "e1_w1": (DIM, HID), "e1_w2": (DIM, HID),
                  "e1_down": (HID, DIM), "e2_l1": (DIM, HID), "e2_l2": (HID, HID), "e2_l3": (HID, HID),
                  "e2_l4": (HID, DIM), "e3_down": (DIM, DIM), "e3_up": (DIM, HID), "e3_out": (HID, DIM)}
        x_parts = names.sb("x_parts", [P, 2, DC, TOKENS], F32R)
        hidden = [names.sb(f"hidden{n}", [P, 2, HID // P, BANK], F32R) for n in range(3)]
        narrow = names.sb("narrow", [P, 2, DIM // P, BANK], F32R)
        layers = [(("e2_l1",), x_parts, hidden[1], ("gelu",)), (("e1_w1", "e1_w2"), x_parts, hidden[0], ("silu", "times")),
                  (("e3_down",), x_parts, narrow, ("gelu",)), (("e2_l2",), hidden[1], hidden[2], ("gelu",)),
                  (("e1_down",), hidden[0], 1, ("out",)), (("e2_l3",), hidden[2], hidden[1], ("gelu",)),
                  (("e3_up",), narrow, hidden[0], ("gelu",)), (("e0_up",), x_parts, hidden[2], ("gelu",)),
                  (("e2_l4",), hidden[1], 2, ("out",)), (("e3_out",), hidden[0], 3, ("out",)),
                  (("e0_down",), hidden[2], 0, ("out",))]
        uses, jobs = [], []
        for batch in range(BATCH):
            for ws, src, dst, kinds in layers:
                for m in range(shapes[ws[0]][1] // P):
                    for k, kind in enumerate(kinds):
                        jobs.append((len(uses) + k, src, dst, kind, batch, m))
                uses += ws
        banks, acted_deep, loaded_deep, parts_deep = 6, 4, 4, 3
        act_jobs = [n for n, job in enumerate(jobs) if job[3] in ("silu", "gelu")]
        dve_jobs = [n for n, job in enumerate(jobs) if job[3] != "silu"]
        last_of = {job[0]: n for n, job in enumerate(jobs)}

        def acted_count(n):
            return sum(j <= n for j in act_jobs)

        def taken_count(n):
            return sum(j <= n for j in dve_jobs)

        def weights_of(u, what):
            n = shapes[uses[u]][0] // P * shapes[uses[u]][1]
            return loaded[:, u % loaded_deep, 0:n] if what == "loaded" else w_parts[:, u % parts_deep, :, 0:n]

        def silu_or_self(n):
            return n + 1 if jobs[n][3] == "silu" else n

        def writer(buffer, before):
            return max((j for j in range(before) if jobs[j][2] is buffer), default=None)

        size = max(rows // P * cols for rows, cols in shapes.values())
        loaded = names.sb("loaded", [P, loaded_deep, size])
        w_parts = names.sb("w_parts", [P, parts_deep, 2, size], F32R)
        acted = names.sb("acted", [P, acted_deep, BANK])
        gate = names.sb("gate", [P, DC, GATES])
        gate_in = names.sem("gate_in")
        weights_in = [names.sem(f"weights_{n}_in") for n in range(loaded_deep)]

        def load(sync, u):
            rows, cols = shapes[uses[u]]
            sync.dma_start(loaded[:, u % loaded_deep, 0:rows // P * cols].rearrange("p (c n) -> p c n", n=cols),
                           dram[f"L1_ffn_{uses[u]}"]).then_inc(weights_in[u % loaded_deep], 16)

        def loads(sync):
            sync.dma_start(gate[:], dram["L1_ffn_gate_w"]).then_inc(gate_in, 16)
            for u in range(loaded_deep):
                load(sync, u)

        norm(nc, "mix_rms", psum, ident, y, DIM, 1.1920929e-07, centre=False, out_feat=xt, gain=gains[:, 1],
             loaded=(gains_in, 16), loads=loads)

        logits = names.sb("logits", [P, TILES, GATES])
        top = names.sb("top", [P, TILES])
        total = names.sb("total", [P, TILES])
        probs = names.sb("probs", [P, TILES, 8])
        best = names.sb("best", [P, TILES, 8])
        which = names.sb("which", [P, TILES, 8], U32)
        which_f = names.sb("which_f", [P, TILES, 2])
        share = names.sb("share", [P, TILES, 2])
        hit = names.sb("hit", [P, 2, TILES, GATES])
        weights = names.sb("weights", [P, TILES, GATES])
        numbers = names.sb("numbers", [P, GATES])
        gate_made, shifted, exped, steps = (names.sem(n) for n in ("gate_made", "shifted", "exped", "steps"))
        numbered, made = names.sem("numbered"), names.sem("made")
        x_high, x_ready = names.sem("x_high"), names.sem("x_ready")
        w_high, w_ready = names.sem("w_high"), names.sem("w_ready")
        acted_ready, taken = names.sem("acted_ready"), names.sem("taken")
        product, product_high = names.sem("product"), names.sem("product_high")
        with nc.Block() as block:
            @block.sync
            def _(sync):
                for u in range(loaded_deep, len(uses)):
                    sync.wait_ge(w_ready, u - loaded_deep + 1)
                    load(sync, u)

            @block.gpsimd
            def _(pool):
                pool.iota(numbers[:], pattern=[[1, GATES]], base=0, channel_multiplier=0,
                          allow_small_or_imprecise_dtypes=True).then_inc(numbered, 1)
                for u in range(len(uses)):
                    src, dst = weights_of(u, "loaded"), weights_of(u, "parts")
                    pool.wait_ge(w_high, u + 1)
                    pool.tensor_tensor(dst[:, 1], src, dst[:, 0].bitcast(F32), ALU.subtract).then_inc(w_ready, 1)

            @block.tensor
            def _(pe):
                pe.wait_ge(gate_in, 16)
                for t in range(TILES):
                    for c in range(DC):
                        last = pe.matmul(bank[7][:, t * GATES:(t + 1) * GATES], xt[:, c, t * P:(t + 1) * P], gate[:, c, :],
                                         start=c == 0, stop=c == DC - 1)
                last.then_inc(gate_made, 1)
                three = ((0, 0), (0, 1), (1, 0))
                for n, (u, src, dst, kind, batch, m) in enumerate(jobs):
                    if n >= banks:
                        before = n - banks
                        if jobs[before][3] == "silu":
                            pe.wait_ge(acted_ready, acted_count(before))
                        else:
                            pe.wait_ge(taken, taken_count(before))
                    pe.wait_ge(w_ready, u + 1)
                    if src is x_parts:
                        pe.wait_ge(x_ready, batch + 1)
                    else:
                        pe.wait_ge(taken, taken_count(writer(src, n)))
                    rows, cols = shapes[uses[u]]
                    chunks = rows // P
                    w = w_parts[:, u % parts_deep, :, 0:chunks * cols].rearrange("p a (c n) -> p a c n", n=cols)
                    first = batch * BANK if src is x_parts else 0
                    terms = [(c, i, j) for c in range(chunks) for i, j in three]
                    for k in range(2 if kind == "out" else 1):
                        for e, (c, i, j) in enumerate(terms):
                            if kind == "out":
                                t = 2 * m + k
                                last = pe.matmul(bank[n % banks][:, k * DIM:(k + 1) * DIM],
                                                 src[:, i, c, t * P:(t + 1) * P], w[:, j, c, :],
                                                 start=e == 0, stop=e == len(terms) - 1)
                            else:
                                last = pe.matmul(bank[n % banks], w[:, i, c, m * P:(m + 1) * P],
                                                 src[:, j, c, first:first + BANK],
                                                 start=e == 0, stop=e == len(terms) - 1)
                    last.then_inc(made, 1)

            @block.scalar
            def _(act):
                def split_rows(batch):
                    cols = slice(batch * BANK, (batch + 1) * BANK)
                    act.activation(x_parts[:, 0, :, cols], xt[:, :, cols], ACT.Copy).then_inc(x_high, 1)

                def split_weights(u):
                    act.wait_ge(weights_in[u % loaded_deep], 16 * (u // loaded_deep + 1))
                    if u >= parts_deep:
                        act.wait_ge(made, last_of[u - parts_deep] + 1)
                    act.activation(weights_of(u, "parts")[:, 0], weights_of(u, "loaded"), ACT.Copy).then_inc(w_high, 1)

                split_rows(0)
                for u in range(parts_deep):
                    split_weights(u)
                split_rows(1)
                split = parts_deep
                act.wait_ge(shifted, 1)
                act.activation(logits[:], logits[:], ACT.Exp).then_inc(exped, 1)
                for k, n in enumerate(act_jobs):
                    _, _, dst, kind, _, m = jobs[n]
                    while split < len(uses) and last_of[split - parts_deep] < n:
                        split_weights(split)
                        split += 1
                    act.wait_ge(made, n + 1)
                    if k >= acted_deep:
                        act.wait_ge(taken, taken_count(silu_or_self(act_jobs[k - acted_deep])))
                    last = act.activation(acted[:, k % acted_deep, :], bank[n % banks],
                                          ACT.Silu if kind == "silu" else ACT.Gelu)
                    if kind == "gelu":
                        last = act.activation(dst[:, 0, m, :], bank[n % banks], ACT.Gelu)
                    last.then_inc(acted_ready, 1)
                for u in range(split, len(uses)):
                    split_weights(u)

            @block.vector
            def _(dve):
                chain = Chain(dve, steps)
                big = 3.4028234663852886e38
                for batch in range(BATCH):
                    cols = slice(batch * BANK, (batch + 1) * BANK)
                    dve.wait_ge(x_high, batch + 1)
                    dve.tensor_tensor(x_parts[:, 1, :, cols], xt[:, :, cols], x_parts[:, 0, :, cols].bitcast(F32),
                                      ALU.subtract).then_inc(x_ready, 1)
                dve.wait_ge(gate_made, 1)
                chain.link(dve.tensor_scalar(logits[:], bank[7][:, 0:TILES * GATES].rearrange("p (t e) -> p t e", e=GATES),
                                             big, -big, ALU.min, ALU.max))
                chain.link(dve.tensor_reduce(top[:], logits[:], AX.X, ALU.max))
                dve.tensor_tensor(logits[:], logits[:], top[:].unsqueeze(2).to_broadcast([P, TILES, GATES]),
                                  ALU.subtract).then_inc(shifted, 1)
                chain.link(dve.memset(probs[:], -1.0))
                dve.wait_ge(exped, 1)
                chain.link(dve.tensor_reduce(total[:], logits[:], AX.X, ALU.add))
                chain.link(dve.reciprocal(total[:], total[:]))
                chain.link(dve.tensor_tensor(probs[:, :, 0:GATES], logits[:],
                                             total[:].unsqueeze(2).to_broadcast([P, TILES, GATES]), ALU.mult))
                for t in range(TILES):
                    last = dve.max(best[:, t, :], probs[:, t, :])
                chain.link(last)
                for t in range(TILES):
                    last = dve.max_index(which[:, t, :], best[:, t, :], probs[:, t, :])
                chain.link(last)
                dve.tensor_copy(which_f[:], which[:, :, 0:2])
                chain.link(dve.tensor_tensor(total[:], best[:, :, 0], best[:, :, 1], ALU.add))
                chain.link(dve.tensor_scalar(total[:], total[:], 1e-8, None, ALU.add))
                chain.link(dve.reciprocal(total[:], total[:]))
                chain.link(dve.tensor_tensor(share[:], best[:, :, 0:2], total[:].unsqueeze(2).to_broadcast([P, TILES, 2]),
                                             ALU.mult))
                dve.wait_ge(numbered, 1)
                for k in range(2):
                    both = [P, TILES, GATES]
                    chain.link(dve.tensor_tensor(hit[:, k], which_f[:, :, k:k + 1].to_broadcast(both),
                                                 numbers[:].unsqueeze(1).to_broadcast(both), ALU.is_equal))
                    chain.link(dve.tensor_tensor(hit[:, k], hit[:, k], share[:, :, k:k + 1].to_broadcast(both), ALU.mult))
                chain.link(dve.tensor_tensor(weights[:], hit[:, 0], hit[:, 1], ALU.add))
                products = 0
                for n in dve_jobs:
                    _, _, dst, kind, batch, m = jobs[n]
                    dve.wait_ge(made, n + 1)
                    if kind == "out":
                        before = [j for j in range(n) if jobs[j][3:] == ("out", batch, m)]
                        if before:
                            dve.wait_ge(taken, taken_count(before[-1]))
                        for k in range(2):
                            t = batch * SEQ_TILES + 2 * m + k
                            last = dve.scalar_tensor_tensor(
                                out=y[:, t, MASKED:], in0=bank[n % banks][:, k * DIM + MASKED:(k + 1) * DIM],
                                scalar=weights[:, t, dst:dst + 1], in1=y[:, t, MASKED:], op0=ALU.mult, op1=ALU.add)
                        last.then_inc(taken, 1)
                        continue
                    values = acted[:, (acted_count(n) - 1) % acted_deep, :]
                    dve.wait_ge(acted_ready, acted_count(n))
                    if kind == "times":
                        products += 1
                        dve.tensor_tensor(values, values, bank[n % banks], ALU.mult).then_inc(product, 1)
                        dve.wait_ge(product, products)
                        dve.tensor_copy(dst[:, 0, m, :], values).then_inc(product_high, 1)
                        dve.wait_ge(product_high, products)
                    dve.tensor_tensor(dst[:, 1, m, :], values, dst[:, 0, m, :].bitcast(F32), ALU.subtract
                                      ).then_inc(taken, 1)
                dve.wait_ge(taken, len(dve_jobs))
                dve.tensor_tensor(x[:], x[:], y[:], ALU.add)


STAGES = [dynamic_conv, cross_attention, product_key_experts, gated_scan, small_cross_attention, last_block]


def build(nc, dram, out):
    with ExitStack() as ctx:
        names = Names(nc, ctx, "all")
        psum = Psum(ctx.enter_context(nc.psum_tensor("psum", [P, 8 * BANK], F32)))
        for name in NORM_SEMS:
            psum.norm_sems[name] = Counted(names.sem(f"norm_{name}"))
        x = names.sb("x", [P, TILES, DIM])
        x_in, stored = names.sem("x_in"), names.sem("stored")
        x_rows = dram["x"].rearrange("(t p) d -> p t d", p=P)
        with nc.Block() as block:
            @block.sync
            def _(sync):
                sync.dma_start(x[:], x_rows).then_inc(x_in, 16)

            @block.vector
            def _(dve):
                dve.wait_ge(x_in, 16)
        ident = constants(nc, names)
        for stage in STAGES:
            before = nc.snapshot_sems()
            stage(nc, dram, psum, ident, x)
            nc.clear_and_free_semaphores(nc.allocated_since(before))
            nc.all_engine_barrier()
        with nc.Block() as block:
            @block.sync
            def _(sync):
                sync.dma_start(out.rearrange("(t p) d -> p t d", p=P), x[:]).then_inc(stored, 16)
                sync.wait_ge(stored, 16)


def _turned(w, kw=P):
    return _chunked(np.ascontiguousarray(w.T), kw)


def _chunked(w, kw=P):
    k, n = w.shape
    return np.ascontiguousarray(w.reshape(k // kw, kw, n).transpose(1, 0, 2))


def _by_feature(v, kw=P):
    return np.ascontiguousarray(v.reshape(-1, kw).T)


def layouts(a):
    out = {"x": a["x"].reshape(TOKENS, DIM)}
    for name in ("w1", "ww", "w2"):
        out[f"L0_attn_{name}"] = _turned(a[f"L0_attn_{name}"])
    for name in ("b1", "bw", "b2", "gamma", "beta"):
        out[f"L0_attn_{name}"] = a[f"L0_attn_{name}"]
    out["ctx"] = a["ctx_768"].reshape(BATCH * KEYS, CTX)
    for name, kw in (("g_x", P), ("b_x", P), ("g_c", CK), ("b_c", CK)):
        out[f"L0_xattn_{name}"] = _by_feature(a[f"L0_xattn_{name}"], kw)
    out["L0_xattn_Wv"] = _chunked(a["L0_xattn_Wv"], CK)
    for name, kw in (("Wq", P), ("Wk", CK)):
        w = a[f"L0_xattn_{name}"]
        out[f"L0_xattn_{name}"] = w.reshape(w.shape[0] // kw, kw, HEADS, WIDE).transpose(2, 1, 0, 3)
    out["L0_xattn_Wo"] = _chunked(a["L0_xattn_Wo"])
    out["L0_ffn_w_q"] = a["L0_ffn_w_q"].reshape(2 * PK_HEADS, PK_DIM, DIM).transpose(1, 0, 2)
    out["L0_ffn_keys_p"] = a["L0_ffn_keys_p"].transpose(3, 2, 0, 1).reshape(PK_DIM, 2 * PK_HEADS, PK_KEYS)
    for name in ("bn_gamma", "bn_beta"):
        out[f"L0_ffn_{name}"] = _by_feature(a[f"L0_ffn_{name}"])
    for name in ("down", "up"):
        w = a[f"L0_ffn_{name}"][:EXPERTS].reshape(PK_KEYS, 2, PK_KEYS // 2, DIM).transpose(2, 1, 0, 3)
        w = w.reshape(EXPERTS, DIM)
        out[f"L0_ffn_{name}"] = _turned(w) if name == "down" else _chunked(w)
    for name in ("ln_z", "dt", "y", "yact"):
        out[f"L1_attn_w_{name}"] = _turned(a[f"L1_attn_w_{name}"])
        out[f"L1_attn_b_{name}"] = _by_feature(a[f"L1_attn_b_{name}"])
    for name in ("w_fc", "w_fcact", "w_out"):
        out[f"L1_attn_{name}"] = _turned(a[f"L1_attn_{name}"])
    out["L1_attn_h0"] = _by_feature(a["L1_attn_h0"])
    out["L1_attn_b_out"] = a["L1_attn_b_out"]
    out["L1_attn_gains"] = np.stack([_by_feature(a["L1_attn_g_sio"]), _by_feature(a["L1_attn_g_ffn"])], 1)
    out["L1_attn_b_ff"] = np.stack([_by_feature(a["L1_attn_b_fc"]), _by_feature(a["L1_attn_b_fcact"])], 1)
    out["ctx_t"] = _turned(out["ctx"], CK)
    out["L1_xattn_kv_w"] = _chunked(a["L1_xattn_kv_w"], CK)
    out["L1_xattn_q_w"] = _chunked(a["L1_xattn_q_w"])
    for name in ("kv_b", "q_b", "proj_b"):
        out[f"L1_xattn_{name}"] = a[f"L1_xattn_{name}"]
    out["L1_xattn_proj_w"] = _chunked(a["L1_xattn_proj_w"])
    out["L1_ffn_gains"] = np.stack([_by_feature(a["L1_ffn_n1_w"]), _by_feature(a["L1_ffn_n2_w"])], 1)
    out["L1_ffn_wqkv"] = np.concatenate([_turned(a[f"L1_ffn_{name}"]) for name in ("wq", "wk", "wv")], axis=2)
    out["L1_ffn_head_gain"] = np.concatenate([a["L1_ffn_qn_w"], a["L1_ffn_kn_w"]])
    out["L1_ffn_wo"] = _turned(a["L1_ffn_wo"])
    for name in ("gate_w", "e0_up", "e0_down", "e1_w1", "e1_w2", "e1_down", "e2_l1", "e2_l2", "e2_l3", "e2_l4",
                 "e3_down", "e3_up", "e3_out"):
        out[f"L1_ffn_{name}"] = _turned(a[f"L1_ffn_{name}"])
    return out


def kernel(**inputs):
    from concourse import bacc as _bacc
    from concourse.bass_utils import run_bass_kernel_spmd as _run

    nc = _bacc.Bacc("TRN2", target_bir_lowering=False, num_devices=1)
    arrays, dram = {}, {}
    for name, a in layouts({k: np.asarray(v) for k, v in inputs.items()}).items():
        a = np.ascontiguousarray(a)
        arrays[f"in_{name}"] = a
        dram[name] = nc.dram_tensor(f"in_{name}", a.shape, mybir.dt.from_np(a.dtype), kind="ExternalInput").ap()
    out = nc.dram_tensor("out_0", (TOKENS, DIM), F32, kind="ExternalOutput").ap()
    build(nc, dram, out)
    result = _run(nc, [arrays], core_ids=[0])
    return result.results[0]["out_0"].reshape(BATCH, SEQ, DIM)
```
